# Optimizing a Trainium2 kernel written in Bass

```python
import numpy as np
import jax
import jax.numpy as jnp

def _softmax(x, axis=-1):
    return jax.nn.softmax(x, axis=axis)

def _gelu(x):
    return jax.nn.gelu(x, approximate=True)

def _silu(x):
    return jax.nn.silu(x)

def _sigmoid(x):
    return jax.nn.sigmoid(x)

def _layernorm(x, axis=-1, eps=1e-05):
    m = jnp.mean(x, axis=axis, keepdims=True)
    v = jnp.var(x, axis=axis, keepdims=True)
    return (x - m) / jnp.sqrt(v + eps)

def _scatter_add(tgt, idx, src, axis=0):
    return tgt.at[idx].add(src)

def _segment_sum(src, seg, n):
    return jax.ops.segment_sum(src, seg, n)
kernel_name = 'mk_audio_tower_d2_tok_audfeat768_r4_9f91c8'

def setup_inputs(seed: int=0):
    np.random.seed(seed)
    _w = jnp.asarray

    def _rec_inputs():
        import jax
        import jax.numpy as jnp
        _rk = jax.random.key(seed)
        x = 0.000106427 + 1.00001 * jax.random.normal(jax.random.fold_in(_rk, 1), (32, 750, 192), jnp.float32)
        return x
    x = _rec_inputs()

    def _L0_tok_setup():
        import jax, jax.numpy as jnp
        import numpy as np
        D_MODEL = 192
        SEGMENT_SIZE = 128
        DILATION_RATE = 2
        key = jax.random.key(seed)
        x = jax.random.normal(key, (4, 4096, D_MODEL), dtype=jnp.float32)
        return {'x': x}
    _L0_tok_all = _L0_tok_setup()
    _L0_tok_in = {k: v for k, v in _L0_tok_all.items() if k in ()}
    del _L0_tok_all

    def _L0_attn_setup():
        import jax, jax.numpy as jnp
        import numpy as np
        B, L, D, M = (1, 512, 192, 64)
        key = jax.random.key(seed)
        ks = jax.random.split(key, 9)

        def w(k, shape):
            return jax.random.normal(k, shape, jnp.float32) * shape[0] ** (-0.5)
        x = jax.random.normal(ks[0], (B, L, D), jnp.float32)
        Wq = w(ks[1], (D, M))
        Wk = w(ks[2], (D, M))
        Wv = w(ks[3], (D, D))
        Wf = w(ks[4], (D, M))
        bf = jnp.zeros((M,), jnp.float32)
        Wo = w(ks[5], (D, D))
        gamma = jnp.ones((D,), jnp.float32)
        beta = jnp.zeros((D,), jnp.float32)
        return {'x': x, 'Wq': Wq, 'Wk': Wk, 'Wv': Wv, 'Wf': Wf, 'bf': bf, 'Wo': Wo, 'gamma': gamma, 'beta': beta}
    _L0_attn_all = _L0_attn_setup()
    _L0_attn_in = {k: v for k, v in _L0_attn_all.items() if k in ('Wq', 'Wk', 'Wv', 'Wf', 'bf', 'Wo', 'gamma', 'beta')}
    del _L0_attn_all

    def _L0_ffn_setup():
        import jax, jax.numpy as jnp
        import numpy as np
        B, S, D = (4, 256, 192)
        E = 8
        H = 192
        HS = 768
        TOPK_ROUTED = 2
        key = jax.random.key(seed)
        ks = jax.random.split(key, 10)
        w = lambda k, shape: jax.random.normal(k, shape, dtype=jnp.float32) * 0.02
        return {'x': jax.random.normal(ks[0], (B, S, D), dtype=jnp.float32), 'router_w': w(ks[1], (D, E)), 'w_gate': w(ks[2], (E, D, H)), 'w_up': w(ks[3], (E, D, H)), 'w_down': w(ks[4], (E, H, D)), 'ws_gate': w(ks[5], (D, HS)), 'ws_up': w(ks[6], (D, HS)), 'ws_down': w(ks[7], (HS, D)), 'sg_w': w(ks[8], (D, 1)), 'sg_b': jnp.zeros((1,), jnp.float32)}
    _L0_ffn_all = _L0_ffn_setup()
    _L0_ffn_in = {k: v for k, v in _L0_ffn_all.items() if k in ('router_w', 'w_gate', 'w_up', 'w_down', 'ws_gate', 'ws_up', 'ws_down', 'sg_w', 'sg_b')}
    del _L0_ffn_all

    def _L1_attn_setup():
        import jax, jax.numpy as jnp
        import numpy as np
        LOG2E = 1.4426950408889634
        NUM_HEADS = 12

        def fake_quant_sym8(x):
            scale = jnp.maximum(jnp.max(jnp.abs(x)) / 127.0, 1e-08)
            q = jnp.clip(jnp.round(x / scale), -128.0, 127.0) * scale
            return x + jax.lax.stop_gradient(q - x)

        def integer_approx_softmax(x):
            z = x * LOG2E
            z = z - jnp.max(z, axis=-1, keepdims=True)
            zi = jnp.floor(z)
            zf = z - zi
            p = jnp.exp2(zi) * (1.0 + zf)
            return p / jnp.sum(p, axis=-1, keepdims=True)
        key = jax.random.key(seed)
        ks = jax.random.split(key, 5)
        B, N, E, P = (8, 256, 192, 192)
        s = 0.02
        return {'x': jax.random.normal(ks[0], (B, N, E), jnp.float32), 'Wq': jax.random.normal(ks[1], (E, P), jnp.float32) * s, 'bq': jnp.zeros((P,), jnp.float32), 'Wk': jax.random.normal(ks[2], (E, P), jnp.float32) * s, 'bk': jnp.zeros((P,), jnp.float32), 'Wv': jax.random.normal(ks[3], (E, P), jnp.float32) * s, 'bv': jnp.zeros((P,), jnp.float32), 'Wo': jax.random.normal(ks[4], (P, E), jnp.float32) * s, 'bo': jnp.zeros((E,), jnp.float32)}
    _L1_attn_all = _L1_attn_setup()
    _L1_attn_in = {k: v for k, v in _L1_attn_all.items() if k in ('Wq', 'bq', 'Wk', 'bk', 'Wv', 'bv', 'Wo', 'bo')}
    del _L1_attn_all

    def _L1_ffn_setup():
        import jax, jax.numpy as jnp
        import numpy as np
        B, S, D_IN, D_HID, D_OUT = (32, 128, 192, 768, 192)
        key = jax.random.key(seed)
        k1, k2, k3, k4 = jax.random.split(key, 4)
        init_k = float(np.sqrt(1.0 / D_IN))
        init_k2 = float(np.sqrt(1.0 / D_HID))
        x = jax.random.normal(k1, (B, S, D_IN), dtype=jnp.float32)
        in_weight = jax.random.uniform(k2, (D_HID, D_IN), dtype=jnp.float32, minval=-init_k, maxval=init_k)
        in_bias = jax.random.uniform(k3, (D_HID,), dtype=jnp.float32, minval=-init_k, maxval=init_k)
        out_weight = jax.random.uniform(k4, (D_HID, D_OUT), dtype=jnp.float32, minval=-init_k2, maxval=init_k2)
        return {'x': x, 'in_weight': in_weight, 'in_bias': in_bias, 'out_weight': out_weight}
    _L1_ffn_all = _L1_ffn_setup()
    _L1_ffn_in = {k: v for k, v in _L1_ffn_all.items() if k in ('in_weight', 'in_bias', 'out_weight')}
    del _L1_ffn_all
    return {'x': x, 'L0_attn_Wq': _L0_attn_in['Wq'], 'L0_attn_Wk': _L0_attn_in['Wk'], 'L0_attn_Wv': _L0_attn_in['Wv'], 'L0_attn_Wf': _L0_attn_in['Wf'], 'L0_attn_bf': _L0_attn_in['bf'], 'L0_attn_Wo': _L0_attn_in['Wo'], 'L0_attn_gamma': _L0_attn_in['gamma'], 'L0_attn_beta': _L0_attn_in['beta'], 'L0_ffn_router_w': _L0_ffn_in['router_w'], 'L0_ffn_w_gate': _L0_ffn_in['w_gate'], 'L0_ffn_w_up': _L0_ffn_in['w_up'], 'L0_ffn_w_down': _L0_ffn_in['w_down'], 'L0_ffn_ws_gate': _L0_ffn_in['ws_gate'], 'L0_ffn_ws_up': _L0_ffn_in['ws_up'], 'L0_ffn_ws_down': _L0_ffn_in['ws_down'], 'L0_ffn_sg_w': _L0_ffn_in['sg_w'], 'L0_ffn_sg_b': _L0_ffn_in['sg_b'], 'L1_attn_Wq': _L1_attn_in['Wq'], 'L1_attn_bq': _L1_attn_in['bq'], 'L1_attn_Wk': _L1_attn_in['Wk'], 'L1_attn_bk': _L1_attn_in['bk'], 'L1_attn_Wv': _L1_attn_in['Wv'], 'L1_attn_bv': _L1_attn_in['bv'], 'L1_attn_Wo': _L1_attn_in['Wo'], 'L1_attn_bo': _L1_attn_in['bo'], 'L1_ffn_in_weight': _L1_ffn_in['in_weight'], 'L1_ffn_in_bias': _L1_ffn_in['in_bias'], 'L1_ffn_out_weight': _L1_ffn_in['out_weight']}

def reference(x, L0_attn_Wq, L0_attn_Wk, L0_attn_Wv, L0_attn_Wf, L0_attn_bf, L0_attn_Wo, L0_attn_gamma, L0_attn_beta, L0_ffn_router_w, L0_ffn_w_gate, L0_ffn_w_up, L0_ffn_w_down, L0_ffn_ws_gate, L0_ffn_ws_up, L0_ffn_ws_down, L0_ffn_sg_w, L0_ffn_sg_b, L1_attn_Wq, L1_attn_bq, L1_attn_Wk, L1_attn_bk, L1_attn_Wv, L1_attn_bv, L1_attn_Wo, L1_attn_bo, L1_ffn_in_weight, L1_ffn_in_bias, L1_ffn_out_weight):
    import jax
    import jax.numpy as jnp

    def _L0_tok_ref(x):
        import jax, jax.numpy as jnp
        import numpy as np
        D_MODEL = 192
        SEGMENT_SIZE = 128
        DILATION_RATE = 2
        B, S, D = x.shape
        pad = -S % SEGMENT_SIZE
        if pad:
            x = jnp.pad(x, ((0, 0), (0, pad), (0, 0)))
        xs = x.reshape(B, -1, SEGMENT_SIZE, D)[:, :, ::DILATION_RATE, :]
        scale = 1.0 / jnp.sqrt(jnp.asarray(D, dtype=x.dtype))
        scores = jnp.einsum('bnqd,bnkd->bnqk', xs, xs) * scale
        attn = jax.nn.softmax(scores, axis=-1)
        out = jnp.einsum('bnqk,bnkd->bnqd', attn, xs)
        return out.reshape(B, -1, D)

    def _L0_attn_ref(x, Wq, Wk, Wv, Wf, bf, Wo, gamma, beta):
        import jax, jax.numpy as jnp
        import numpy as np
        B, L, D, M = (1, 512, 192, 64)
        m_dim = Wq.shape[1]
        scale = m_dim ** (-0.5)
        q = (jax.nn.elu(x @ Wq) + 1.0) * scale
        k = jax.nn.elu(x @ Wk) + 1.0
        v = x @ Wv
        forget = jax.nn.sigmoid(x @ Wf + bf)
        log_f = jnp.log(jnp.clip(forget, 1e-06, None))
        log_f_cum = jnp.clip(jnp.cumsum(log_f, axis=1), -20.0, 20.0)
        exp_neg = jnp.exp(-log_f_cum)
        exp_pos = jnp.exp(log_f_cum)
        kv = k[..., :, None] * v[..., None, :]
        cum_kv = jnp.cumsum(exp_neg[..., None] * kv, axis=1)
        Mstate = exp_pos[..., None] * cum_kv
        z = exp_pos * jnp.cumsum(exp_neg * k, axis=1)
        numerator = jnp.einsum('blm,blmd->bld', q, Mstate)
        denominator = jnp.einsum('blm,blm->bl', q, z)[..., None] + 1e-06
        h = numerator / denominator
        mu = jnp.mean(h, axis=-1, keepdims=True)
        var = jnp.var(h, axis=-1, keepdims=True)
        normed = (h - mu) / jnp.sqrt(var + 1e-05) * gamma + beta
        return normed @ Wo

    def _L0_ffn_ref(x, router_w, w_gate, w_up, w_down, ws_gate, ws_up, ws_down, sg_w, sg_b):
        import jax, jax.numpy as jnp
        import numpy as np
        B, S, D = (4, 256, 192)
        E = 8
        H = 192
        HS = 768
        TOPK_ROUTED = 2
        probs = jax.nn.softmax(x @ router_w, axis=-1)
        gates, idx = jax.lax.top_k(probs, TOPK_ROUTED)
        gates = gates / jnp.sum(gates, axis=-1, keepdims=True)
        n_exp = router_w.shape[1]
        dense_g = jnp.sum(jax.nn.one_hot(idx, n_exp, dtype=x.dtype) * gates[..., None], axis=-2)
        g = jax.nn.silu(jnp.einsum('bsd,edh->bseh', x, w_gate))
        u = jnp.einsum('bsd,edh->bseh', x, w_up)
        expert_out = jnp.einsum('bseh,ehd->bsed', g * u, w_down)
        routed = jnp.einsum('bse,bsed->bsd', dense_g, expert_out)
        shared = jax.nn.silu(x @ ws_gate) * (x @ ws_up) @ ws_down
        alpha = jax.nn.sigmoid(x @ sg_w + sg_b)
        return alpha * shared + (1.0 - alpha) * routed

    def _L1_attn_ref(x, Wq, bq, Wk, bk, Wv, bv, Wo, bo):
        import jax, jax.numpy as jnp
        import numpy as np
        LOG2E = 1.4426950408889634
        NUM_HEADS = 12

        def fake_quant_sym8(x):
            scale = jnp.maximum(jnp.max(jnp.abs(x)) / 127.0, 1e-08)
            q = jnp.clip(jnp.round(x / scale), -128.0, 127.0) * scale
            return x + jax.lax.stop_gradient(q - x)

        def integer_approx_softmax(x):
            z = x * LOG2E
            z = z - jnp.max(z, axis=-1, keepdims=True)
            zi = jnp.floor(z)
            zf = z - zi
            p = jnp.exp2(zi) * (1.0 + zf)
            return p / jnp.sum(p, axis=-1, keepdims=True)
        B, N, E = x.shape
        H = NUM_HEADS
        D = Wq.shape[1] // H
        xq = fake_quant_sym8(x)
        Q = (xq @ Wq + bq).reshape(B, N, H, D).transpose(0, 2, 1, 3)
        K = (xq @ Wk + bk).reshape(B, N, H, D).transpose(0, 2, 1, 3)
        V = (xq @ Wv + bv).reshape(B, N, H, D).transpose(0, 2, 1, 3)
        logits = jnp.einsum('bhnd,bhmd->bhnm', Q, K)
        attn = integer_approx_softmax(logits)
        ctx = jnp.einsum('bhnm,bhmd->bhnd', attn, V)
        ctx = ctx.transpose(0, 2, 1, 3).reshape(B, N, H * D)
        return ctx @ Wo + bo

    def _L1_ffn_ref(x, in_weight, in_bias, out_weight):
        import jax, jax.numpy as jnp
        import numpy as np
        B, S, D_IN, D_HID, D_OUT = (32, 128, 192, 768, 192)
        lead = x.shape[:-1]
        xt = x.reshape(-1, in_weight.shape[1])
        h = jax.nn.gelu(jnp.einsum('td,hd->th', xt, in_weight) + in_bias, approximate=False)
        out = jnp.einsum('th,ho->to', h, out_weight)
        return out.reshape(*lead, out_weight.shape[1])
    h = _L0_tok_ref(x)
    h = h + _L0_attn_ref(_layernorm(h, axis=-1), L0_attn_Wq, L0_attn_Wk, L0_attn_Wv, L0_attn_Wf, L0_attn_bf, L0_attn_Wo, L0_attn_gamma, L0_attn_beta)
    h = h + _L0_ffn_ref(_layernorm(h, axis=-1), L0_ffn_router_w, L0_ffn_w_gate, L0_ffn_w_up, L0_ffn_w_down, L0_ffn_ws_gate, L0_ffn_ws_up, L0_ffn_ws_down, L0_ffn_sg_w, L0_ffn_sg_b)
    h = h + _L1_attn_ref(_layernorm(h, axis=-1), L1_attn_Wq, L1_attn_bq, L1_attn_Wk, L1_attn_bk, L1_attn_Wv, L1_attn_bv, L1_attn_Wo, L1_attn_bo)
    h = h + _L1_ffn_ref(_layernorm(h, axis=-1), L1_ffn_in_weight, L1_ffn_in_bias, L1_ffn_out_weight)
    return h

_drawn_inputs = setup_inputs


def setup_inputs(seed=0):
    import zlib

    import numpy as np

    out = dict(_drawn_inputs(seed))
    spreads = {'L0_attn_bf': (0.0, 0.749),
     'L0_attn_gamma': (1.0, 0.2),
     'L0_attn_beta': (0.0, 0.1),
     'L1_attn_bq': (0.0, 2.0),
     'L1_attn_bk': (0.0, 2.0),
     'L1_attn_bv': (0.0, 2.0),
     'L1_attn_bo': (0.0, 0.665)}
    factors = {'L0_attn_Wf': 3.079,
     'L0_ffn_router_w': 8.0,
     'L0_ffn_w_gate': 8.0,
     'L0_ffn_w_up': 8.0,
     'L0_ffn_w_down': 8.0,
     'L0_ffn_ws_gate': 7.528,
     'L0_ffn_ws_up': 7.445,
     'L0_ffn_ws_down': 7.486,
     'L0_ffn_sg_w': 8.0,
     'L1_attn_Wq': 54.141,
     'L1_attn_Wk': 53.414,
     'L1_ffn_in_bias': 28.644,
     'L1_attn_Wv': 6.394,
     'L1_attn_Wo': 3.202}
    for name, (base, spread) in spreads.items():
        noise = np.random.default_rng([zlib.crc32(name.encode()), seed]).standard_normal(out[name].shape)
        drawn = base * np.exp(spread * noise) if base else spread * noise
        out[name] = jnp.asarray(drawn.astype(out[name].dtype))
    for name, factor in factors.items():
        out[name] = (out[name] * factor).astype(out[name].dtype)
    return out
```

```python
from contextlib import ExitStack

import concourse.bass as bass
from concourse import mybir

ALU = mybir.AluOpType
ACT = mybir.ActivationFunctionType
AX = mybir.AxisListType
F32 = mybir.dt.float32
F16 = mybir.dt.float16
BF16 = mybir.dt.bfloat16
I32 = mybir.dt.int32
U32 = mybir.dt.uint32
RMAX = bass.bass_isa.ReduceOp.max

P = 128
HALF = 64
NT = 3
N = NT * P
D = 192
M0 = 64
E0 = 8
HT0 = (E0 * D + 768) // P
RT0 = E0 * D // P
NGATE = RT0 + 1
HT1 = 768 // P
NH = 12
DH = D // NH
NG = NH // 2
VW = DH + 1
LOG2E = 1.4426950408889634
BITS = float(1 << 23)
ROUND = 1.5 * BITS
MAXSCALE = 64.0

C_QK = 0
C_F = C_QK + 2 * M0
C_V = C_F + 2 * M0
C_R = C_V + D
RW = 16
C_GU = C_R + RW
C_IN = C_GU + HT0 * 2 * P
WCOLS = C_IN + HT1 * P
C_KS = NG * P
C_V1 = 2 * NG * P
QCOLS = C_V1 + D

K_ID, K_MASK, K_SGN, K_TERMQ, K_TERMK, K_QSC, K_IOTA = 0, 128, 256, 257, 258, 259, 260
KCOLS = K_IOTA + E0
V_BF, V_GA, V_BA, V_GB, V_BB, V_SG, V_IN, V_BQ, V_BK, V_BV, V_BO = 0, 1, 2, 3, 4, 5, 6, 12, 18, 24, 216
VCOLS = V_BO + D


class Signal:

    def __init__(self, sem, per_batch, base=0):
        self.sem, self.per_batch, self.base = sem, per_batch, base

    def nth(self, b, k=None):
        return b * self.per_batch + (self.base + self.per_batch if k is None else self.base + k)

    def before(self, b):
        assert self.base > 0
        return b * self.per_batch + self.base


def tower(nc, x, w_a, w_b, wq_a, wq_b, w_down0, w_out1, w_o, consts, params, sel, out):
    B, S, _ = x.shape
    LAST = (S - 4 * P + 1) // 2
    h3_dram = nc.dram_tensor("h3_scratch", (B, P, NT, D), F32).ap()

    ctx = ExitStack()
    with ctx:
        def sb(name, shape, dt=F32):
            return ctx.enter_context(nc.sbuf_tensor(name, shape, dt))

        based = []

        def sig(name, per_batch=1, base=0):
            made = Signal(ctx.enter_context(nc.semaphore(name)), per_batch, base)
            if base:
                based.append(made)
            return made

        passed = ctx.enter_context(nc.semaphore("passed"))

        def stand(eng):
            eng.sem_inc(passed, 1)

        wa_hi, wa_lo, wb_hi = (sb(n, [P, WCOLS], F16) for n in ("wa_hi", "wa_lo", "wb_hi"))
        wb_lo = sb("wb_lo", [HALF, WCOLS], F16)
        qa_hi, qa_lo, qb_hl = (sb(n, [P, QCOLS], F16) for n in ("qa_hi", "qa_lo", "qb_hl"))
        wdown0 = sb("wdown0", [P, HT0, D])
        wout1 = sb("wout1", [P, HT1, D])
        wo = sb("wo", [P, 4, D])
        cst = sb("cst", [P, KCOLS])
        par = sb("par", [P, VCOLS])
        selb = sb("selb", [32, NGATE, P], BF16)
        self32 = sb("self32", [32, NGATE, P])
        neg_bf = sb("neg_bf", [P, 1])
        neg_sg = sb("neg_sg", [P, 1])
        id16 = sb("id16", [P, P], F16)
        idb = sb("idb", [P, P], BF16)
        ones = sb("ones", [P, N])
        neghalf = sb("neghalf", [P, NT])
        ident = cst[:, K_ID:K_ID + P]
        mask = cst[:, K_MASK:K_MASK + P]

        xin = sb("xin", [P, NT, D])
        xs = sb("xs", [P, NT, D])
        xsT_a = sb("xsT_a", [P, N])
        xsT_b = sb("xsT_b", [HALF, N])
        prob = sb("prob", [P, NT, P])
        probT = sb("probT", [P, NT, P])
        rowmax = sb("rowmax", [P, NT])
        rowsum = sb("rowsum", [P, NT])
        rowinv = sb("rowinv", [P, NT])
        h1 = sb("h1", [P, NT, D])
        h2 = sb("h2", [P, NT, D])
        h3 = sb("h3", [P, NT, D])
        st = sb("st", [P, NT, 6])
        mv = sb("mv", [P, NT, 2])
        var_eps = sb("var_eps", [P, NT])
        rstd = sb("rstd", [P, NT])
        xn = sb("xn", [P, NT, D])
        xa_hi, xa_lo, xb = (sb(n, [P, N], F16) for n in ("xa_hi", "xa_lo", "xb"))
        forget = sb("forget", [P, N])
        decay = sb("decay", [P, N])
        qk_min = sb("qk_min", [P, N])
        qk = sb("qk", [P, N])
        qd = sb("qd", [M0, N])
        kd = sb("kd", [M0, N])
        vals = sb("vals", [P, NT, D + 1])
        att = sb("att", [P, NT, N])
        den = sb("den", [P, NT])
        deninv = sb("deninv", [P, NT])
        hn = sb("hn", [P, NT, D])
        hnT_a = sb("hnT_a", [P, N])
        hnT_b = sb("hnT_b", [HALF, N])
        logit = sb("logit", [P, NT, E0])
        top = sb("top", [P, NT, 8])
        top_i = sb("top_i", [P, NT, 8], U32)
        top_f = sb("top_f", [P, NT, 2])
        gexp = sb("gexp", [P, NT, 2])
        gden = sb("gden", [P, NT, 2])
        grec = sb("grec", [P, NT, 2])
        gw2 = sb("gw2", [P, NT, 2])
        hot = sb("hot", [P, NT, 2, E0])
        gate9 = sb("gate9", [P, NT, 9])
        gres = sb("gres", [P, NT, 9])
        gsplit = sb("gsplit", [P, NT, 32], BF16)
        gateT = sb("gateT", [32, N], BF16)
        gates = sb("gates", [P, NGATE, N])
        silu = sb("silu", [P, 2, N])
        gu = sb("gu", [P, 2, N])
        hid = sb("hid", [P, 3, N])
        absmax = sb("absmax", [P, 2])
        stat3 = sb("stat3", [P, B * NT, 2])
        rstd3 = sb("rstd3", [P, B * NT])
        allmax = sb("allmax", [P, 1])
        qscale = sb("qscale", [P, 1])
        qinv = sb("qinv", [P, 1])
        qnat = sb("qnat", [P, NT, D], F16)
        qT_a = sb("qT_a", [P, N], F16)
        qT_b = sb("qT_b", [P, N], F16)
        sfull = silu
        shi = sb("shi", [P, 2, N], F16)
        stacks = sb("stacks", [P, 2 * NG, N], F16)
        v1 = sb("v1", [P, NT, NH * VW])
        negmax = sb("negmax", [P, NT * NH])
        nmf = sb("nmf", [P, NT * NH])
        nmr = sb("nmr", [P, NT * NH])
        nm = sb("nm", [P, NT, NH * HALF], F16)
        pT = gates[:, 0:2 * NT, :].bitcast(I32)
        csum = sb("csum", [P, NT, NH])
        cx = hn
        hbo = h3
        h4 = sb("h4", [P, NT, D])
        ho = sb("ho", [P, NT, D])

        ps = ctx.enter_context(nc.psum_tensor("ps", [P, 8, 512], F32))
        F = [ps[:, 0, :], ps[:, 1, :]]
        F3 = ps[:, 0:2, :].rearrange("p a (c n) -> p (a c) n", n=256)[:, 0:NT, :]
        G = [ps[:, 2, :], ps[:, 3, :]]
        U = [ps[:, 4, :], ps[:, 5, :]]
        D3 = ps[:, 6:8, :].rearrange("p a (c n) -> p (a c) n", n=256)[:, 0:NT, :]

        def f16_bank(i):
            return ps[:, i, :].bitcast(F16)

        def cols(t, k=1):
            return slice(t * P, (t + k) * P)

        def split_terms(act, c, m):
            s = slice(c, c + m)
            return [(act[0], wa_hi[:, s]), (act[0], wa_lo[:, s]), (act[1], wa_hi[:, s]),
                    (act[2], wb_hi[:, s]), (act[2][0:HALF], wb_lo[:, s])]

        def weights_stationary(out_, act, c, m):
            terms = split_terms(act, c, m)
            for i, (a, w) in enumerate(terms):
                last = nc.tensor.matmul(out_, w, a, start=i == 0, stop=i == len(terms) - 1)
            return last

        def tokens_stationary(out_, act, c, m, t, first=True):
            terms = split_terms(act, c, m)
            for i, (a, w) in enumerate(terms):
                last = nc.tensor.matmul(out_, a[:, cols(t)], w, start=i == 0, stop=i == len(terms) - 1)
            return last

        X = (xa_hi[:], xa_lo[:], xb[:])

        CH = 1168
        chunks = [(w_a, w_b, c, min(CH, WCOLS - c), False) for c in range(0, WCOLS, CH)]
        chunks += [(wq_a, wq_b, c, min(CH, QCOLS - c), True) for c in range(0, QCOLS, CH)]
        stage = gates[:].rearrange("p a n -> p (a n)")

        def staged(n, half, w):
            at = ((n % 2) * 2 + half) * CH
            return stage[:, at:at + w]

        s_const = sig("const_landed", 5 * 16)
        s_weights = sig("weights_landed", 3 * 16)
        s_stage = [sig("staged_even", 32), sig("staged_odd", 32)]
        s_hi = sig("weights_hi", 2)
        s_lo = sig("weights_lo", 2)
        s_prep = sig("prepared", 6)
        s_mem = sig("cleared", 8)

        with nc.Block() as block:
            @block.sync
            def _(sp):
                sp.dma_start(cst[:], consts).then_inc(s_const.sem, 16)
                sp.dma_start(par[:], params).then_inc(s_const.sem, 16)
                sp.dma_start(self32[:], sel).then_inc(s_const.sem, 16)
                for n, (a, b_, c, w, _) in enumerate(chunks):
                    if n >= 2:
                        sp.wait_ge(s_hi.sem, s_hi.nth(n - 2))
                        sp.wait_ge(s_lo.sem, s_lo.nth(n - 2))
                    sp.dma_start(staged(n, 0, w), a[:, c:c + w]).then_inc(s_stage[n % 2].sem, 16)
                    sp.dma_start(staged(n, 1, w), b_[:, c:c + w]).then_inc(s_stage[n % 2].sem, 16)
                sp.dma_start(wdown0[:], w_down0).then_inc(s_weights.sem, 16)
                sp.dma_start(wout1[:], w_out1).then_inc(s_weights.sem, 16)
                sp.dma_start(wo[:], w_o).then_inc(s_weights.sem, 16)
                sp.wait_ge(s_weights.sem, s_weights.nth(0))

            @block.scalar
            def _(act):
                for n, (_, _, c, w, quant) in enumerate(chunks):
                    act.wait_ge(s_stage[n % 2].sem, s_stage[n % 2].nth(n // 2))
                    hi, b_hi = (qa_hi, qb_hl) if quant else (wa_hi, wb_hi)
                    nc.scalar.activation(hi[:, c:c + w], staged(n, 0, w), ACT.Copy).then_inc(s_hi.sem, 1)
                    nc.scalar.activation(b_hi[:, c:c + w], staged(n, 1, w), ACT.Copy).then_inc(s_hi.sem, 1)

            @block.vector
            def _(dve):
                for n, (_, _, c, w, quant) in enumerate(chunks):
                    s = slice(c, c + w)
                    dve.wait_ge(s_hi.sem, s_hi.nth(n))
                    hi, lo = (qa_hi, qa_lo) if quant else (wa_hi, wa_lo)
                    nc.vector.tensor_tensor(lo[:, s], staged(n, 0, w), hi[:, s], ALU.subtract).then_inc(s_lo.sem, 1)
                    if quant:
                        nc.vector.tensor_tensor(qb_hl[HALF:P, s], staged(n, 1, w)[HALF:P], qb_hl[HALF:P, s],
                                                ALU.subtract).then_inc(s_lo.sem, 1)
                    else:
                        nc.vector.tensor_tensor(wb_lo[:, s], staged(n, 1, w)[0:HALF], wb_hi[0:HALF, s],
                                                ALU.subtract).then_inc(s_lo.sem, 1)
                dve.wait_ge(s_const.sem, s_const.nth(0, 3 * 16))
                nc.vector.tensor_copy(id16[:], ident).then_inc(s_prep.sem, 1)
                nc.vector.tensor_copy(idb[:], ident).then_inc(s_prep.sem, 1)
                nc.vector.tensor_copy(selb[:], self32[:]).then_inc(s_prep.sem, 1)
                nc.vector.tensor_scalar(neg_bf[:], par[:, V_BF:V_BF + 1], -1.0, None, ALU.mult).then_inc(s_prep.sem, 1)
                nc.vector.tensor_scalar(neg_sg[:], par[:, V_SG:V_SG + 1], -1.0, None, ALU.mult).then_inc(s_prep.sem, 1)
                nc.vector.memset(absmax[:], 0.0).then_inc(s_prep.sem, 1)

            @block.gpsimd
            def _(pool):
                nc.gpsimd.memset(xin[:], 0.0).then_inc(s_mem.sem, 1)
                nc.gpsimd.memset(ones[:], 1.0).then_inc(s_mem.sem, 1)
                nc.gpsimd.memset(neghalf[:], -0.5).then_inc(s_mem.sem, 1)
                nc.gpsimd.memset(prob[:], 0.0).then_inc(s_mem.sem, 1)
                nc.gpsimd.memset(vals[:, :, D:D + 1], 1.0).then_inc(s_mem.sem, 1)
                nc.gpsimd.memset(gsplit[:], 0.0).then_inc(s_mem.sem, 1)
                nc.gpsimd.memset(nm[:], 0.0).then_inc(s_mem.sem, 1)
                nc.gpsimd.memset(v1[:], 1.0).then_inc(s_mem.sem, 1)

        x_landed = sig("x_landed", 32)
        xs_ready = sig("xs_ready", base=1)
        xsT_psum = sig("xsT_psum", 2)
        xsTa_ready = sig("xsTa_ready")
        xsTb_ready = sig("xsTb_ready")
        scores0 = sig("scores0")
        max0 = sig("max0", 2)
        shifted0 = sig("shifted0", 2)
        exp0 = sig("exp0", 2)
        sum0 = sig("sum0", 3)
        probT_psum = sig("probT_psum")
        probT_ready = sig("probT_ready")
        tok_psum = sig("tok_psum", base=1)
        h1_ready = sig("h1_ready")
        ln_stat = sig("ln_stat", 4 * 2)
        ln_eps = sig("ln_eps", 4)
        ln_rstd = sig("ln_rstd", 4)
        xn_ready = sig("xn_ready", 4)
        xnT_psum = sig("xnT_psum", 3 * 2)
        x_hi = sig("x_hi", 2 * 2)
        x_lo = sig("x_lo", 2 * 2)
        qk_psum = sig("qk_psum")
        f_psum = sig("f_psum")
        fexp = sig("fexp")
        fcap = sig("fcap")
        flog = sig("flog")
        fcum = sig("fcum", 2)
        decay_ready = sig("decay_ready")
        qkmin_ready = sig("qkmin_ready")
        qkexp = sig("qkexp")
        qk_ready = sig("qk_ready")
        decayed = sig("decayed", 2)
        v_psum = sig("v_psum")
        v_ready = sig("v_ready")
        att_psum = sig("att_psum")
        att_diag = sig("att_diag", NT)
        att_off = sig("att_off", 2)
        num_psum = sig("num_psum")
        den_ready = sig("den_ready", 2)
        hn_ready = sig("hn_ready")
        hnTa_ready = sig("hnTa_ready")
        hnTb_ready = sig("hnTb_ready")
        wo_psum = sig("wo_psum")
        h2_ready = sig("h2_ready")
        route_psum = sig("route_psum")
        logit_ready = sig("logit_ready", 2)
        top_ready = sig("top_ready", NT)
        topi_ready = sig("topi_ready", NT)
        topf_ready = sig("topf_ready", 2)
        gexp_ready = sig("gexp_ready", 2)
        gate_step = sig("gate_step", 11)
        gateT_psum = sig("gateT_psum")
        gateT_ready = sig("gateT_ready")
        bcast_psum = sig("bcast_psum", NGATE)
        gate_ready = sig("gate_ready", NGATE, base=1)
        g_psum = sig("g_psum", HT0)
        u_psum = sig("u_psum", HT0)
        silu_ready = sig("silu_ready", HT0)
        gu_ready = sig("gu_ready", HT0)
        hid_ready = sig("hid_ready", HT0)
        down_done = sig("down_done", HT0)
        h3_ready = sig("h3_ready", base=1)
        absmax_step = sig("absmax_step", 2)
        stat_kept = sig("stat_kept", 2, base=1)
        h3_stored = sig("h3_stored", 16, base=16)

        with nc.Block() as block:
            @block.sync
            def _(sp):
                for made in based:
                    sp.sem_inc(made.sem, made.base)
                based.clear()

        with nc.Block() as block:
            @block.sync
            def _(sp):
                with sp.Fori(0, B) as b:
                    sp.wait_ge(xs_ready.sem, xs_ready.before(b))
                    even = x[b, 0:4 * P:2, :].rearrange("(t p) d -> p t d", p=P)
                    sp.dma_start(xin[:, 0:2, :], even).then_inc(x_landed.sem, 16)
                    sp.dma_start(xin[0:LAST, 2, :], x[b, 4 * P:S:2, :]).then_inc(x_landed.sem, 16)
                    sp.wait_ge(h3_ready.sem, h3_ready.nth(b))
                    sp.dma_start(h3_dram[b], h3[:]).then_inc(h3_stored.sem, 16)
                sp.wait_ge(h3_stored.sem, h3_stored.nth(B - 1))

            @block.gpsimd
            def _(pool):
                def rstd_of(b, n):
                    pool.wait_ge(ln_stat.sem, ln_stat.nth(b, 2 * n + 2))
                    stand(pool)
                    nc.gpsimd.tensor_scalar(var_eps[:], mv[:, :, 1], 1e-5, None, ALU.add).then_inc(ln_eps.sem, 1)
                    pool.wait_ge(ln_eps.sem, ln_eps.nth(b, n + 1))
                    nc.gpsimd.tensor_tensor(rstd[:], var_eps[:], neghalf[:], ALU.pow).then_inc(ln_rstd.sem, 1)

                with pool.Fori(0, B) as b:
                    pool.wait_ge(x_landed.sem, x_landed.nth(b))
                    pool.wait_ge(tok_psum.sem, tok_psum.before(b))
                    stand(pool)
                    nc.gpsimd.tensor_copy(xs[:], xin[:]).then_inc(xs_ready.sem, 1)
                    for n in range(4):
                        rstd_of(b, n)
                    pool.wait_ge(ln_rstd.sem, ln_rstd.nth(b))
                    stand(pool)
                    nc.gpsimd.tensor_copy(stat3[:, bass.ds(b * NT, NT), :], mv[:]).then_inc(stat_kept.sem, 1)
                    nc.gpsimd.tensor_copy(rstd3[:, bass.ds(b * NT, NT)], rstd[:]).then_inc(stat_kept.sem, 1)

            @block.tensor
            def _(pe):
                def transposes(src, done):
                    for t in range(NT):
                        last = nc.tensor.transpose(F[0][:, cols(t)], src[:, t, 0:P], ident)
                    last.then_inc(done.sem, 1)
                    for t in range(NT):
                        last = nc.tensor.transpose(F[1][0:HALF, cols(t)], src[:, t, P:D], ident)
                    last.then_inc(done.sem, 1)

                with pe.Fori(0, B) as b:
                    pe.wait_ge(xs_ready.sem, xs_ready.nth(b))
                    pe.wait_ge(gate_ready.sem, gate_ready.before(b))
                    transposes(xs, xsT_psum)
                    pe.wait_ge(xsTa_ready.sem, xsTa_ready.nth(b))
                    pe.wait_ge(xsTb_ready.sem, xsTb_ready.nth(b))
                    for t in range(NT):
                        nc.tensor.matmul(F[0][:, cols(t)], xsT_a[:, cols(t)], xsT_a[:, cols(t)], start=True, stop=False)
                        last = nc.tensor.matmul(F[0][:, cols(t)], xsT_b[:, cols(t)], xsT_b[:, cols(t)], start=False, stop=True)
                    last.then_inc(scores0.sem, 1)
                    pe.wait_ge(exp0.sem, exp0.nth(b))
                    for t in range(NT):
                        last = nc.tensor.transpose(F[1][:, cols(t)], prob[:, t, :], ident)
                    last.then_inc(probT_psum.sem, 1)
                    pe.wait_ge(probT_ready.sem, probT_ready.nth(b))
                    for t in range(NT):
                        last = nc.tensor.matmul(F3[:, t, 0:D], probT[:, t, :], xs[:, t, :], start=True, stop=True)
                    last.then_inc(tok_psum.sem, 1)

                    pe.wait_ge(xn_ready.sem, xn_ready.nth(b, 1))
                    transposes(xn, xnT_psum)
                    pe.wait_ge(x_hi.sem, x_hi.nth(b, 2))
                    pe.wait_ge(x_lo.sem, x_lo.nth(b, 2))
                    weights_stationary(F[1][:, 0:N], X, C_F, P).then_inc(f_psum.sem, 1)
                    weights_stationary(F[0][:, 0:N], X, C_QK, P).then_inc(qk_psum.sem, 1)
                    pe.wait_ge(fexp.sem, fexp.nth(b))
                    pe.wait_ge(qk_ready.sem, qk_ready.nth(b))
                    for t in range(NT):
                        last = tokens_stationary(F3[:, t, 0:D], X, C_V, D, t)
                    last.then_inc(v_psum.sem, 1)
                    pe.wait_ge(v_ready.sem, v_ready.nth(b))
                    pe.wait_ge(decayed.sem, decayed.nth(b))
                    nc.tensor.matmul(F[0][:, 0:N], kd[:, cols(0)], qd[:], start=True, stop=True)
                    nc.tensor.matmul(F[1][:, 0:2 * P], kd[:, cols(1)], qd[:, cols(1, 2)], start=True, stop=True)
                    nc.tensor.matmul(F[1][:, 2 * P:3 * P], kd[:, cols(2)], qd[:, cols(2)],
                                     start=True, stop=True).then_inc(att_psum.sem, 1)
                    pe.wait_ge(att_diag.sem, att_diag.nth(b))
                    pe.wait_ge(att_off.sem, att_off.nth(b))
                    for t in range(NT):
                        for j in range(t + 1):
                            last = nc.tensor.matmul(F3[:, t, 0:D + 1], att[:, j, cols(t)], vals[:, j, :],
                                                    start=j == 0, stop=j == t)
                    last.then_inc(num_psum.sem, 1)
                    pe.wait_ge(xn_ready.sem, xn_ready.nth(b, 2))
                    transposes(xn, xnT_psum)
                    pe.wait_ge(hnTa_ready.sem, hnTa_ready.nth(b))
                    pe.wait_ge(hnTb_ready.sem, hnTb_ready.nth(b))
                    for t in range(NT):
                        nc.tensor.matmul(F3[:, t, 0:D], hnT_a[:, cols(t)], wo[:, 0, :], start=True, stop=False)
                        last = nc.tensor.matmul(F3[:, t, 0:D], hnT_b[:, cols(t)], wo[0:HALF, 1, :],
                                                start=False, stop=True)
                    last.then_inc(wo_psum.sem, 1)

                    pe.wait_ge(xn_ready.sem, xn_ready.nth(b, 3))
                    transposes(xn, xnT_psum)
                    pe.wait_ge(x_hi.sem, x_hi.nth(b))
                    pe.wait_ge(x_lo.sem, x_lo.nth(b))
                    for t in range(NT):
                        last = tokens_stationary(F[0][:, t * RW:t * RW + RW], X, C_R, RW, t)
                    last.then_inc(route_psum.sem, 1)
                    pe.wait_ge(gate_step.sem, gate_step.nth(b))
                    gT = ps[:, 1, :].bitcast(BF16)
                    for t in range(NT):
                        last = nc.tensor.transpose(gT[0:32, cols(t)], gsplit[:, t, :], idb[:])
                    last.then_inc(gateT_psum.sem, 1)
                    pe.wait_ge(gateT_ready.sem, gateT_ready.nth(b))
                    for i in range(NGATE):
                        if i >= 2:
                            pe.wait_ge(gate_ready.sem, gate_ready.nth(b, i - 1))
                        nc.tensor.matmul(F[i % 2][:, 0:N], selb[:, i, :], gateT[:],
                                         start=True, stop=True).then_inc(bcast_psum.sem, 1)

                    pe.wait_ge(h3_ready.sem, h3_ready.before(b))
                    for i in range(HT0 + 2):
                        if i < HT0:
                            c = C_GU + 2 * P * i
                            if i >= 2:
                                pe.wait_ge(silu_ready.sem, silu_ready.nth(b, i - 1))
                            weights_stationary(G[i % 2][:, 0:N], X, c, P).then_inc(g_psum.sem, 1)
                            if i >= 2:
                                pe.wait_ge(gu_ready.sem, gu_ready.nth(b, i - 1))
                            weights_stationary(U[i % 2][:, 0:N], X, c + P, P).then_inc(u_psum.sem, 1)
                        j = i - 2
                        if j >= 0:
                            pe.wait_ge(hid_ready.sem, hid_ready.nth(b, j + 1))
                            for t in range(NT):
                                last = nc.tensor.matmul(D3[:, t, 0:D], hid[:, j % 3, cols(t)], wdown0[:, j, :],
                                                        start=j == 0 and t != 1, stop=j == HT0 - 1,
                                                        skip_group_check=True)
                            last.then_inc(down_done.sem, 1)

            @block.scalar
            def _(act):
                with act.Fori(0, B) as b:
                    act.wait_ge(xsT_psum.sem, xsT_psum.nth(b, 1))
                    nc.scalar.activation(xsT_a[:], F[0][:, 0:N], ACT.Copy).then_inc(xsTa_ready.sem, 1)
                    for s in range(2):
                        r = slice(s * HALF, (s + 1) * HALF)
                        act.wait_ge(shifted0.sem, shifted0.nth(b, s + 1))
                        nc.scalar.activation(prob[r, :, r], prob[r, :, r], ACT.Exp,
                                             scale=float(D) ** -0.5).then_inc(exp0.sem, 1)
                    act.wait_ge(probT_psum.sem, probT_psum.nth(b))
                    nc.scalar.activation(probT[:], F[1][:, 0:N].rearrange("p (t n) -> p t n", t=NT),
                                         ACT.Copy).then_inc(probT_ready.sem, 1)
                    act.wait_ge(xnT_psum.sem, xnT_psum.nth(b, 1))
                    nc.scalar.activation(xa_hi[:], F[0][:, 0:N], ACT.Copy).then_inc(x_hi.sem, 1)
                    act.wait_ge(xnT_psum.sem, xnT_psum.nth(b, 2))
                    nc.scalar.activation(xb[0:HALF], F[1][0:HALF, 0:N], ACT.Copy).then_inc(x_hi.sem, 1)
                    act.wait_ge(f_psum.sem, f_psum.nth(b))
                    nc.scalar.activation(forget[:], F[1][:, 0:N], ACT.Exp, scale=-1.0,
                                         bias=neg_bf[:]).then_inc(fexp.sem, 1)
                    act.wait_ge(qkmin_ready.sem, qkmin_ready.nth(b))
                    nc.scalar.activation(qk_min[:], qk_min[:], ACT.Exp).then_inc(qkexp.sem, 1)
                    act.wait_ge(fcap.sem, fcap.nth(b))
                    nc.scalar.activation(forget[:], forget[:], ACT.Ln).then_inc(flog.sem, 1)
                    act.wait_ge(fcum.sem, fcum.nth(b))
                    nc.scalar.activation(decay[:], decay[:], ACT.Exp,
                                         scale=cst[:, K_SGN:K_SGN + 1]).then_inc(decay_ready.sem, 1)
                    act.wait_ge(v_psum.sem, v_psum.nth(b))
                    nc.scalar.activation(vals[:, :, 0:D], F3[:, :, 0:D], ACT.Copy).then_inc(v_ready.sem, 1)
                    act.wait_ge(att_psum.sem, att_psum.nth(b))
                    act.wait_ge(att_diag.sem, att_diag.nth(b, 1))
                    nc.scalar.activation(att[:, 0, cols(1, 2)], F[0][:, cols(1, 2)], ACT.Copy).then_inc(att_off.sem, 1)
                    act.wait_ge(att_diag.sem, att_diag.nth(b))
                    nc.scalar.activation(att[:, 1, cols(2)], F[1][:, cols(1)], ACT.Copy).then_inc(att_off.sem, 1)
                    act.wait_ge(xnT_psum.sem, xnT_psum.nth(b, 3))
                    nc.scalar.activation(hnT_a[:], F[0][:, 0:N], ACT.Identity, scale=par[:, V_GA:V_GA + 1],
                                         bias=par[:, V_BA:V_BA + 1]).then_inc(hnTa_ready.sem, 1)
                    act.wait_ge(xnT_psum.sem, xnT_psum.nth(b, 5))
                    nc.scalar.activation(xa_hi[:], F[0][:, 0:N], ACT.Copy).then_inc(x_hi.sem, 1)
                    act.wait_ge(xnT_psum.sem, xnT_psum.nth(b, 6))
                    nc.scalar.activation(xb[0:HALF], F[1][0:HALF, 0:N], ACT.Copy).then_inc(x_hi.sem, 1)
                    act.wait_ge(topf_ready.sem, topf_ready.nth(b))
                    nc.scalar.activation(gexp[:, :, 0], gexp[:, :, 0], ACT.Exp).then_inc(gexp_ready.sem, 1)
                    nc.scalar.activation(gexp[:, :, 1], gexp[:, :, 1], ACT.Exp, scale=-1.0,
                                         bias=neg_sg[:]).then_inc(gexp_ready.sem, 1)
                    act.wait_ge(gateT_psum.sem, gateT_psum.nth(b))
                    nc.scalar.activation(gateT[:], ps[:, 1, :].bitcast(BF16)[0:32, 0:N], ACT.Copy).then_inc(gateT_ready.sem, 1)
                    for i in range(NGATE):
                        act.wait_ge(bcast_psum.sem, bcast_psum.nth(b, i + 1))
                        nc.scalar.activation(gates[:, i, :], F[i % 2][:, 0:N], ACT.Copy).then_inc(gate_ready.sem, 1)
                    for i in range(HT0):
                        act.wait_ge(g_psum.sem, g_psum.nth(b, i + 1))
                        if i >= 2:
                            act.wait_ge(gu_ready.sem, gu_ready.nth(b, i - 1))
                        nc.scalar.activation(silu[:, i % 2, :], G[i % 2][:, 0:N], ACT.Silu).then_inc(silu_ready.sem, 1)

            @block.vector
            def _(dve):
                def norm_stats(b, n, src):
                    if n == 0:
                        dve.wait_ge(stat_kept.sem, stat_kept.before(b))
                    for t in range(NT):
                        last = nc.vector.bn_stats(st[:, t, :], src[:, t, :])
                    last.then_inc(ln_stat.sem, 1)
                    dve.wait_ge(ln_stat.sem, ln_stat.nth(b, 2 * n + 1))
                    stand(dve)
                    for t in range(NT):
                        last = nc.vector.bn_aggr(mv[:, t, :], st[:, t, :])
                    last.then_inc(ln_stat.sem, 1)

                def normalise(b, n, src):
                    dve.wait_ge(ln_rstd.sem, ln_rstd.nth(b, n + 1))
                    for t in range(NT):
                        last = nc.vector.tensor_scalar(xn[:, t, :], src[:, t, :], mv[:, t, 0:1], rstd[:, t:t + 1],
                                                       ALU.subtract, ALU.mult)
                    last.then_inc(xn_ready.sem, 1)

                def split_low(b, k):
                    dve.wait_ge(x_hi.sem, x_hi.nth(b, 2 * k + 1))
                    nc.vector.tensor_tensor(xa_lo[:], F[0][:, 0:N], xa_hi[:], ALU.subtract).then_inc(x_lo.sem, 1)
                    dve.wait_ge(x_hi.sem, x_hi.nth(b, 2 * k + 2))
                    nc.vector.tensor_tensor(xb[HALF:P], F[1][0:HALF, 0:N], xb[0:HALF], ALU.subtract).then_inc(x_lo.sem, 1)

                S0 = F[0][:, 0:N].rearrange("p (t n) -> p t n", t=NT)
                with dve.Fori(0, B) as b:
                    dve.wait_ge(xsT_psum.sem, xsT_psum.nth(b, 2))
                    nc.vector.tensor_copy(xsT_b[:], F[1][0:HALF, 0:N]).then_inc(xsTb_ready.sem, 1)
                    dve.wait_ge(scores0.sem, scores0.nth(b))
                    halves = [slice(0, HALF), slice(HALF, P)]
                    for r in halves:
                        nc.vector.tensor_reduce(rowmax[r], S0[r, :, r], AX.X, ALU.max).then_inc(max0.sem, 1)
                    for s, r in enumerate(halves):
                        dve.wait_ge(max0.sem, max0.nth(b, s + 1))
                        nc.vector.tensor_tensor(prob[r, :, r], S0[r, :, r],
                                                rowmax[r].unsqueeze(2).broadcast_to([HALF, NT, HALF]),
                                                ALU.subtract).then_inc(shifted0.sem, 1)
                    for s, r in enumerate(halves):
                        dve.wait_ge(exp0.sem, exp0.nth(b, s + 1))
                        nc.vector.tensor_reduce(rowsum[r], prob[r, :, r], AX.X, ALU.add).then_inc(sum0.sem, 1)
                    dve.wait_ge(sum0.sem, sum0.nth(b, 2))
                    nc.vector.reciprocal(rowinv[:], rowsum[:]).then_inc(sum0.sem, 1)
                    dve.wait_ge(sum0.sem, sum0.nth(b))
                    dve.wait_ge(tok_psum.sem, tok_psum.nth(b))
                    nc.vector.tensor_tensor(h1[:], F3[:, :, 0:D], rowinv[:].unsqueeze(2).broadcast_to([P, NT, D]),
                                            ALU.mult).then_inc(h1_ready.sem, 1)
                    dve.wait_ge(h1_ready.sem, h1_ready.nth(b))
                    norm_stats(b, 0, h1)
                    normalise(b, 0, h1)
                    split_low(b, 0)

                    dve.wait_ge(fexp.sem, fexp.nth(b))
                    nc.vector.tensor_scalar(forget[:], forget[:], 1.0, 1e6, ALU.add, ALU.min).then_inc(fcap.sem, 1)
                    dve.wait_ge(qk_psum.sem, qk_psum.nth(b))
                    nc.vector.tensor_scalar(qk_min[:], F[0][:, 0:N], 0.0, None, ALU.min).then_inc(qkmin_ready.sem, 1)
                    dve.wait_ge(qkexp.sem, qkexp.nth(b))
                    nc.vector.scalar_tensor_tensor(qk[:], F[0][:, 0:N], 0.0, qk_min[:], ALU.max,
                                                   ALU.add).then_inc(qk_ready.sem, 1)
                    dve.wait_ge(flog.sem, flog.nth(b))
                    nc.vector.tensor_tensor_scan(decay[:], ones[:], forget[:], 0.0, ALU.mult, ALU.add).then_inc(fcum.sem, 1)
                    dve.wait_ge(fcum.sem, fcum.nth(b, 1))
                    nc.vector.tensor_scalar(decay[:], decay[:], 20.0, -20.0, ALU.min, ALU.max).then_inc(fcum.sem, 1)
                    dve.wait_ge(qk_ready.sem, qk_ready.nth(b))
                    dve.wait_ge(decay_ready.sem, decay_ready.nth(b))
                    nc.vector.scalar_tensor_tensor(qd[:], qk[0:M0], float(M0) ** -0.5, decay[0:M0], ALU.mult,
                                                   ALU.mult).then_inc(decayed.sem, 1)
                    nc.vector.tensor_tensor(kd[:], qk[M0:P], decay[M0:P], ALU.mult).then_inc(decayed.sem, 1)
                    dve.wait_ge(att_psum.sem, att_psum.nth(b))
                    for j in range(NT):
                        src = F[0][:, cols(0)] if j == 0 else F[1][:, cols(2 * (j - 1))]
                        nc.vector.tensor_tensor(att[:, j, cols(j)], src, mask, ALU.mult).then_inc(att_diag.sem, 1)
                    dve.wait_ge(num_psum.sem, num_psum.nth(b))
                    nc.vector.tensor_scalar(den[:], F3[:, :, D], 1e-6, None, ALU.add).then_inc(den_ready.sem, 1)
                    dve.wait_ge(den_ready.sem, den_ready.nth(b, 1))
                    nc.vector.reciprocal(deninv[:], den[:]).then_inc(den_ready.sem, 1)
                    dve.wait_ge(den_ready.sem, den_ready.nth(b, 2))
                    nc.vector.tensor_tensor(hn[:], F3[:, :, 0:D], deninv[:].unsqueeze(2).broadcast_to([P, NT, D]),
                                            ALU.mult).then_inc(hn_ready.sem, 1)
                    dve.wait_ge(hn_ready.sem, hn_ready.nth(b))
                    norm_stats(b, 1, hn)
                    normalise(b, 1, hn)
                    dve.wait_ge(xnT_psum.sem, xnT_psum.nth(b, 4))
                    nc.vector.tensor_scalar(hnT_b[:], F[1][0:HALF, 0:N], par[0:HALF, V_GB:V_GB + 1],
                                            par[0:HALF, V_BB:V_BB + 1], ALU.mult, ALU.add).then_inc(hnTb_ready.sem, 1)
                    dve.wait_ge(wo_psum.sem, wo_psum.nth(b))
                    nc.vector.tensor_tensor(h2[:], F3[:, :, 0:D], h1[:], ALU.add).then_inc(h2_ready.sem, 1)
                    dve.wait_ge(h2_ready.sem, h2_ready.nth(b))
                    norm_stats(b, 2, h2)
                    normalise(b, 2, h2)
                    split_low(b, 1)

                    dve.wait_ge(route_psum.sem, route_psum.nth(b))
                    R = F[0][:, 0:NT * RW].rearrange("p (t n) -> p t n", t=NT)
                    nc.vector.tensor_copy(logit[:], R[:, :, 0:E0]).then_inc(logit_ready.sem, 1)
                    nc.vector.tensor_copy(gexp[:, :, 1], R[:, :, E0]).then_inc(logit_ready.sem, 1)
                    dve.wait_ge(logit_ready.sem, logit_ready.nth(b, 1))
                    stand(dve)
                    for t in range(NT):
                        nc.vector.max(top[:, t, :], logit[:, t, :]).then_inc(top_ready.sem, 1)
                    for t in range(NT):
                        dve.wait_ge(top_ready.sem, top_ready.nth(b, t + 1))
                        stand(dve)
                        nc.vector.max_index(top_i[:, t, :], top[:, t, :], logit[:, t, :]).then_inc(topi_ready.sem, 1)
                    dve.wait_ge(topi_ready.sem, topi_ready.nth(b))
                    nc.vector.tensor_tensor(gexp[:, :, 0], top[:, :, 1], top[:, :, 0], ALU.subtract).then_inc(topf_ready.sem, 1)
                    nc.vector.tensor_copy(top_f[:], top_i[:, :, 0:2]).then_inc(topf_ready.sem, 1)
                    k = 0

                    def step(ins):
                        nonlocal k
                        k += 1
                        ins.then_inc(gate_step.sem, 1)
                        dve.wait_ge(gate_step.sem, gate_step.nth(b, k))

                    iota = cst[:, K_IOTA:K_IOTA + E0].unsqueeze(1).broadcast_to([P, NT, E0])
                    dve.wait_ge(gexp_ready.sem, gexp_ready.nth(b))
                    step(nc.vector.tensor_scalar(gden[:], gexp[:], 1.0, None, ALU.add))
                    step(nc.vector.reciprocal(grec[:], gden[:]))
                    nc.vector.tensor_copy(gate9[:, :, E0], grec[:, :, 1])
                    step(nc.vector.tensor_scalar(gden[:, :, 1], grec[:, :, 1], -1.0, 1.0, ALU.mult, ALU.add))
                    step(nc.vector.tensor_tensor(gw2[:, :, 0], grec[:, :, 0], gden[:, :, 1], ALU.mult))
                    nc.vector.tensor_tensor(gw2[:, :, 1], gw2[:, :, 0], gexp[:, :, 0], ALU.mult)
                    for i in range(2):
                        last = nc.vector.tensor_tensor(hot[:, :, i, :], iota,
                                                       top_f[:, :, i].unsqueeze(2).broadcast_to([P, NT, E0]), ALU.is_equal)
                    step(last)
                    for i in range(2):
                        last = nc.vector.tensor_tensor(hot[:, :, i, :], hot[:, :, i, :],
                                                       gw2[:, :, i].unsqueeze(2).broadcast_to([P, NT, E0]), ALU.mult)
                    step(last)
                    step(nc.vector.tensor_tensor(gate9[:, :, 0:E0], hot[:, :, 0, :], hot[:, :, 1, :], ALU.add))
                    step(nc.vector.tensor_copy(gsplit[:, :, 0:9], gate9[:]))
                    step(nc.vector.tensor_tensor(gres[:], gate9[:], gsplit[:, :, 0:9], ALU.subtract))
                    step(nc.vector.tensor_copy(gsplit[:, :, 9:18], gres[:]))
                    step(nc.vector.tensor_tensor(gsplit[:, :, 18:27], gres[:], gsplit[:, :, 9:18], ALU.subtract))
                    assert k == gate_step.per_batch

                    for i in range(HT0 + 1):
                        if i < HT0:
                            dve.wait_ge(silu_ready.sem, silu_ready.nth(b, i + 1))
                            dve.wait_ge(u_psum.sem, u_psum.nth(b, i + 1))
                            if i >= 2:
                                dve.wait_ge(hid_ready.sem, hid_ready.nth(b, i - 1))
                            nc.vector.tensor_tensor(gu[:, i % 2, :], U[i % 2][:, 0:N], silu[:, i % 2, :],
                                                    ALU.mult).then_inc(gu_ready.sem, 1)
                        j = i - 1
                        if j >= 0:
                            dve.wait_ge(gu_ready.sem, gu_ready.nth(b, j + 1))
                            dve.wait_ge(gate_ready.sem, gate_ready.nth(b))
                            if j >= 3:
                                dve.wait_ge(down_done.sem, down_done.nth(b, j - 2))
                            nc.vector.tensor_tensor(hid[:, j % 3, :], gu[:, j % 2, :], gates[:, min(j, RT0), :],
                                                    ALU.mult).then_inc(hid_ready.sem, 1)
                    dve.wait_ge(down_done.sem, down_done.nth(b))
                    dve.wait_ge(h3_stored.sem, h3_stored.before(b))
                    nc.vector.tensor_tensor(h3[:], D3[:, :, 0:D], h2[:], ALU.add).then_inc(h3_ready.sem, 1)
                    dve.wait_ge(h3_ready.sem, h3_ready.nth(b))
                    norm_stats(b, 3, h3)
                    normalise(b, 3, h3)
                    dve.wait_ge(xn_ready.sem, xn_ready.nth(b))
                    nc.vector.tensor_reduce(absmax[:, 1:2], xn[:], AX.XY, ALU.max,
                                            apply_absolute_value=True).then_inc(absmax_step.sem, 1)
                    dve.wait_ge(absmax_step.sem, absmax_step.nth(b, 1))
                    nc.vector.tensor_tensor(absmax[:, 0:1], absmax[:, 0:1], absmax[:, 1:2], ALU.max).then_inc(absmax_step.sem, 1)

        S = [ps[:, i, 0:N] for i in range(3)]
        T = [ps[:, i, 0:N] for i in range(3, 6)]
        W = [ps[:, i, 0:N] for i in range(6, 8)]
        W3 = D3
        h3_landed = sig("h3_landed", 16)
        allmax_ready = sig("allmax_ready")
        qscale_ready = sig("qscale_ready", 2)
        h3_copied = sig("h3_copied", 4, base=1)
        xn3_ready = sig("xn3_ready", 3)
        qnat_ready = sig("qnat_ready")
        qT_psum = sig("qT_psum", 2)
        qTa_ready = sig("qTa_ready", 2)
        qTb_ready = sig("qTb_ready")
        stack_psum = sig("stack_psum", 2 * NG)
        shi_ready = sig("shi_ready", 2 * NG)
        sfull_ready = sig("sfull_ready", 2 * NG)
        stack_ready = sig("stack_ready", 2 * NG)
        v1_psum = sig("v1_psum")
        v1_ready = sig("v1_ready")
        s_psum = sig("s_psum", NH * NT)
        max_ready = sig("max_ready", NH * NT)
        nm_step = sig("nm_step", 5)
        nmT_psum = sig("nmT_psum", NG)
        shifted1 = sig("shifted1", NG)
        sT_psum = sig("sT_psum", NH * NT)
        p_ready = sig("p_ready", NH * NT)
        pv_done = sig("pv_done", NH)
        csum_ready = sig("csum_ready")
        cx_ready = sig("cx_ready")
        cxT_psum = sig("cxT_psum", 2)
        cxTa_ready = sig("cxTa_ready")
        cxTb_ready = sig("cxTb_ready")
        wo1_psum = sig("wo1_psum")
        h4_ready = sig("h4_ready", base=1)
        ln4_stat = sig("ln4_stat", 2)
        ln4_eps = sig("ln4_eps")
        ln4_rstd = sig("ln4_rstd")
        xn4_ready = sig("xn4_ready", base=1)
        xn4T_psum = sig("xn4T_psum", 2)
        x4_hi = sig("x4_hi", 2)
        x4_lo = sig("x4_lo", 2)
        in_psum = sig("in_psum", HT1)
        gelu_ready = sig("gelu_ready", HT1)
        out_done = sig("out_done", HT1)
        ho_ready = sig("ho_ready", base=1)
        out_stored = sig("out_stored", 16, base=16)

        with nc.Block() as block:
            @block.sync
            def _(sp):
                for made in based:
                    sp.sem_inc(made.sem, made.base)

        with nc.Block() as block:
            @block.sync
            def _(sp):
                with sp.Fori(0, B) as b:
                    sp.wait_ge(h3_copied.sem, h3_copied.before(b))
                    sp.dma_start(h1[:], h3_dram[b]).then_inc(h3_landed.sem, 16)
                    sp.wait_ge(ho_ready.sem, ho_ready.nth(b))
                    sp.dma_start(out[b].rearrange("(t p) d -> p t d", p=P), ho[:]).then_inc(out_stored.sem, 16)
                sp.wait_ge(out_stored.sem, out_stored.nth(B - 1))

            @block.gpsimd
            def _(pool):
                nc.gpsimd.partition_all_reduce(allmax[:], absmax[:, 0:1], P, RMAX).then_inc(allmax_ready.sem, 1)
                with pool.Fori(0, B) as b:
                    pool.wait_ge(h3_landed.sem, h3_landed.nth(b))
                    pool.wait_ge(h4_ready.sem, h4_ready.before(b))
                    stand(pool)
                    nc.gpsimd.tensor_copy(h2[:], h1[:]).then_inc(h3_copied.sem, 1)
                    nc.gpsimd.tensor_tensor(hbo[:], h1[:], par[:, V_BO:V_BO + D].unsqueeze(1).broadcast_to([P, NT, D]),
                                            ALU.add).then_inc(h3_copied.sem, 1)
                    pool.wait_ge(xn4_ready.sem, xn4_ready.before(b))
                    stand(pool)
                    nc.gpsimd.tensor_copy(mv[:], stat3[:, bass.ds(b * NT, NT), :]).then_inc(h3_copied.sem, 1)
                    nc.gpsimd.tensor_copy(rstd[:], rstd3[:, bass.ds(b * NT, NT)]).then_inc(h3_copied.sem, 1)
                    pool.wait_ge(ln4_stat.sem, ln4_stat.nth(b))
                    stand(pool)
                    nc.gpsimd.tensor_scalar(var_eps[:], mv[:, :, 1], 1e-5, None, ALU.add).then_inc(ln4_eps.sem, 1)
                    pool.wait_ge(ln4_eps.sem, ln4_eps.nth(b))
                    nc.gpsimd.tensor_tensor(rstd[:], var_eps[:], neghalf[:], ALU.pow).then_inc(ln4_rstd.sem, 1)

            @block.tensor
            def _(pe):
                with pe.Fori(0, B) as b:
                    pe.wait_ge(qnat_ready.sem, qnat_ready.nth(b))
                    qA, qB = ps[:, 0, :].bitcast(F16), ps[:, 1, :].bitcast(F16)
                    for t in range(NT):
                        last = nc.tensor.transpose(qA[:, cols(t)], qnat[:, t, 0:P], id16[:])
                    last.then_inc(qT_psum.sem, 1)
                    for t in range(NT):
                        last = nc.tensor.transpose(qB[0:HALF, cols(t)], qnat[:, t, P:D], id16[:])
                    last.then_inc(qT_psum.sem, 1)
                    pe.wait_ge(qTa_ready.sem, qTa_ready.nth(b))
                    pe.wait_ge(qTb_ready.sem, qTb_ready.nth(b))
                    pe.wait_ge(ho_ready.sem, ho_ready.before(b))
                    for i in range(2 * NG):
                        if i >= 2:
                            pe.wait_ge(sfull_ready.sem, sfull_ready.nth(b, i - 1))
                        s = slice(i * P, (i + 1) * P)
                        nc.tensor.matmul(W[i % 2], qa_hi[:, s], qT_a[:], start=True, stop=False)
                        nc.tensor.matmul(W[i % 2], qa_lo[:, s], qT_a[:], start=False, stop=False)
                        nc.tensor.matmul(W[i % 2], qb_hl[:, s], qT_b[:], start=False, stop=True).then_inc(stack_psum.sem, 1)
                    pe.wait_ge(sfull_ready.sem, sfull_ready.nth(b))
                    s = slice(C_V1, C_V1 + D)
                    for t in range(NT):
                        nc.tensor.matmul(W3[:, t, 0:D], qT_a[:, cols(t)], qa_hi[:, s], start=True, stop=False)
                        nc.tensor.matmul(W3[:, t, 0:D], qT_a[:, cols(t)], qa_lo[:, s], start=False, stop=False)
                        last = nc.tensor.matmul(W3[:, t, 0:D], qT_b[:, cols(t)], qb_hl[:, s], start=False, stop=True)
                    last.then_inc(v1_psum.sem, 1)
                    for h in range(NH):
                        r = slice((h % 2) * HALF, (h % 2 + 1) * HALF)
                        if h % 2 == 0:
                            pe.wait_ge(stack_ready.sem, stack_ready.nth(b, NG + h // 2 + 1))
                        for t in range(NT):
                            if h > 0:
                                pe.wait_ge(max_ready.sem, max_ready.nth(b, (h - 1) * NT + t + 1))
                            nc.tensor.matmul(S[t], stacks[r, h // 2, cols(t)], stacks[r, NG + h // 2, :],
                                             start=True, stop=True).then_inc(s_psum.sem, 1)
                    pe.wait_ge(nm_step.sem, nm_step.nth(b))
                    pe.wait_ge(v1_ready.sem, v1_ready.nth(b))
                    for g in range(NG):
                        if g >= 2:
                            pe.wait_ge(shifted1.sem, shifted1.nth(b, g - 1))
                        for t in range(NT):
                            last = nc.tensor.matmul(W[g % 2][:, cols(t)], nm[:, t, g * P:(g + 1) * P], id16[:],
                                                    start=True, stop=True)
                        last.then_inc(nmT_psum.sem, 1)
                    pe.wait_ge(shifted1.sem, shifted1.nth(b))
                    for h in range(NH + 1):
                        if h < NH:
                            r = slice((h % 2) * HALF, (h % 2 + 1) * HALF)
                            for m in range(NT):
                                if h > 0:
                                    pe.wait_ge(p_ready.sem, p_ready.nth(b, (h - 1) * NT + m + 1))
                                nc.tensor.matmul(T[m], stacks[r, NG + h // 2, cols(m)], stacks[r, h // 2, :],
                                                 start=True, stop=True).then_inc(sT_psum.sem, 1)
                        if h > 0:
                            g = h - 1
                            pe.wait_ge(p_ready.sem, p_ready.nth(b, g * NT + NT))
                            for n in range(NT):
                                for m in range(NT):
                                    w = pT[:, (g % 2) * NT + m, cols(n)].bitcast(F32)
                                    last = nc.tensor.matmul(W3[:, n, g * VW:(g + 1) * VW], w, v1[:, m, g * VW:(g + 1) * VW],
                                                            start=m == 0, stop=m == NT - 1)
                            last.then_inc(pv_done.sem, 1)
                    pe.wait_ge(cx_ready.sem, cx_ready.nth(b))
                    for t in range(NT):
                        last = nc.tensor.transpose(F[0][:, cols(t)], cx[:, t, 0:P], ident)
                    last.then_inc(cxT_psum.sem, 1)
                    for t in range(NT):
                        last = nc.tensor.transpose(F[1][0:HALF, cols(t)], cx[:, t, P:D], ident)
                    last.then_inc(cxT_psum.sem, 1)
                    pe.wait_ge(cxTa_ready.sem, cxTa_ready.nth(b))
                    pe.wait_ge(cxTb_ready.sem, cxTb_ready.nth(b))
                    for t in range(NT):
                        nc.tensor.matmul(F3[:, t, 0:D], hnT_a[:, cols(t)], wo[:, 2, :], start=True, stop=False)
                        last = nc.tensor.matmul(F3[:, t, 0:D], hnT_b[:, cols(t)], wo[0:HALF, 3, :], start=False, stop=True)
                    last.then_inc(wo1_psum.sem, 1)
                    pe.wait_ge(xn4_ready.sem, xn4_ready.nth(b))
                    for t in range(NT):
                        last = nc.tensor.transpose(F[0][:, cols(t)], xn[:, t, 0:P], ident)
                    last.then_inc(xn4T_psum.sem, 1)
                    for t in range(NT):
                        last = nc.tensor.transpose(F[1][0:HALF, cols(t)], xn[:, t, P:D], ident)
                    last.then_inc(xn4T_psum.sem, 1)
                    pe.wait_ge(x4_hi.sem, x4_hi.nth(b))
                    pe.wait_ge(x4_lo.sem, x4_lo.nth(b))
                    for i in range(HT1 + 2):
                        if i < HT1:
                            if i >= 3:
                                pe.wait_ge(gelu_ready.sem, gelu_ready.nth(b, i - 2))
                            weights_stationary(T[i % 3], X, C_IN + i * P, P).then_inc(in_psum.sem, 1)
                        j = i - 2
                        if j >= 0:
                            pe.wait_ge(gelu_ready.sem, gelu_ready.nth(b, j + 1))
                            for t in range(NT):
                                last = nc.tensor.matmul(W3[:, t, 0:D], hid[:, j % 3, cols(t)], wout1[:, j, :],
                                                        start=j == 0 and t != 1, stop=j == HT1 - 1,
                                                        skip_group_check=True)
                            last.then_inc(out_done.sem, 1)

            @block.scalar
            def _(act):
                act.wait_ge(qscale_ready.sem, qscale_ready.nth(0))
                with act.Fori(0, B) as b:
                    act.wait_ge(qT_psum.sem, qT_psum.nth(b, 1))
                    nc.scalar.activation(qT_a[:], ps[:, 0, :].bitcast(F16)[:, 0:N], ACT.Copy).then_inc(qTa_ready.sem, 1)
                    act.wait_ge(qT_psum.sem, qT_psum.nth(b, 2))
                    nc.scalar.activation(qT_b[0:HALF], ps[:, 1, :].bitcast(F16)[0:HALF, 0:N], ACT.Copy).then_inc(qTa_ready.sem, 1)
                    for i in range(2 * NG):
                        act.wait_ge(stack_psum.sem, stack_psum.nth(b, i + 1))
                        if i >= 2:
                            act.wait_ge(stack_ready.sem, stack_ready.nth(b, i - 1))
                        nc.scalar.activation(sfull[:, i % 2, :], W[i % 2], ACT.Identity, scale=qscale[:],
                                             bias=par[:, V_BQ + i:V_BQ + i + 1]).then_inc(sfull_ready.sem, 1)
                    for h in range(NH):
                        for m in range(NT):
                            act.wait_ge(sT_psum.sem, sT_psum.nth(b, h * NT + m + 1))
                            if h >= 2:
                                act.wait_ge(pv_done.sem, pv_done.nth(b, h - 1))
                            nc.scalar.activation(pT[:, (h % 2) * NT + m, :], T[m], ACT.Relu, scale=LOG2E * BITS,
                                                 bias=cst[:, K_QSC:K_QSC + 1]).then_inc(p_ready.sem, 1)
                    act.wait_ge(cxT_psum.sem, cxT_psum.nth(b, 1))
                    nc.scalar.activation(hnT_a[:], F[0][:, 0:N], ACT.Copy).then_inc(cxTa_ready.sem, 1)
                    act.wait_ge(xn4T_psum.sem, xn4T_psum.nth(b, 1))
                    nc.scalar.activation(xa_hi[:], F[0][:, 0:N], ACT.Copy).then_inc(x4_hi.sem, 1)
                    act.wait_ge(xn4T_psum.sem, xn4T_psum.nth(b, 2))
                    nc.scalar.activation(xb[0:HALF], F[1][0:HALF, 0:N], ACT.Copy).then_inc(x4_hi.sem, 1)
                    for i in range(HT1):
                        act.wait_ge(in_psum.sem, in_psum.nth(b, i + 1))
                        if i >= 3:
                            act.wait_ge(out_done.sem, out_done.nth(b, i - 2))
                        nc.scalar.activation(hid[:, i % 3, :], T[i % 3], ACT.Gelu,
                                             bias=par[:, V_IN + i:V_IN + i + 1]).then_inc(gelu_ready.sem, 1)

            @block.vector
            def _(dve):
                dve.wait_ge(allmax_ready.sem, allmax_ready.nth(0))
                nc.vector.tensor_scalar(qscale[:], allmax[:], 1.0 / 127.0, 1e-8, ALU.mult, ALU.max).then_inc(qscale_ready.sem, 1)
                dve.wait_ge(qscale_ready.sem, qscale_ready.nth(0, 1))
                nc.vector.reciprocal(qinv[:], qscale[:]).then_inc(qscale_ready.sem, 1)
                dve.wait_ge(qscale_ready.sem, qscale_ready.nth(0))
                with dve.Fori(0, B) as b:
                    dve.wait_ge(h3_copied.sem, h3_copied.nth(b))
                    for t in range(NT):
                        last = nc.vector.tensor_scalar(xn[:, t, :], h2[:, t, :], mv[:, t, 0:1], rstd[:, t:t + 1],
                                                       ALU.subtract, ALU.mult)
                    last.then_inc(xn3_ready.sem, 1)
                    dve.wait_ge(xn3_ready.sem, xn3_ready.nth(b, 1))
                    nc.vector.tensor_scalar(xn[:], xn[:], qinv[:], 127.0, ALU.mult, ALU.min).then_inc(xn3_ready.sem, 1)
                    dve.wait_ge(xn3_ready.sem, xn3_ready.nth(b, 2))
                    nc.vector.tensor_scalar(xn[:], xn[:], -128.0, ROUND, ALU.max, ALU.add).then_inc(xn3_ready.sem, 1)
                    dve.wait_ge(xn3_ready.sem, xn3_ready.nth(b, 3))
                    nc.vector.tensor_scalar(qnat[:], xn[:], ROUND, None, ALU.subtract).then_inc(qnat_ready.sem, 1)
                    dve.wait_ge(qTa_ready.sem, qTa_ready.nth(b))
                    nc.vector.tensor_copy(qT_b[HALF:P], qT_b[0:HALF]).then_inc(qTb_ready.sem, 1)
                    for i in range(2 * NG + 1):
                        if i < 2 * NG:
                            dve.wait_ge(sfull_ready.sem, sfull_ready.nth(b, i + 1))
                            nc.vector.tensor_copy(shi[:, i % 2, :], sfull[:, i % 2, :]).then_inc(shi_ready.sem, 1)
                        j = i - 1
                        if j >= 0:
                            term = K_TERMQ if j < NG else K_TERMK
                            dve.wait_ge(shi_ready.sem, shi_ready.nth(b, j + 1))
                            nc.vector.scalar_tensor_tensor(stacks[:, j, :], shi[:, j % 2, :], cst[:, term:term + 1],
                                                           sfull[:, j % 2, :], ALU.mult, ALU.add).then_inc(stack_ready.sem, 1)
                    dve.wait_ge(v1_psum.sem, v1_psum.nth(b))
                    for t in range(NT):
                        last = nc.vector.scalar_tensor_tensor(
                            v1[:, t, :].rearrange("p (h c) -> p h c", c=VW)[:, :, 0:DH],
                            W3[:, t, 0:D].rearrange("p (h c) -> p h c", c=DH), qscale[:],
                            par[:, V_BV:V_BV + D].rearrange("p (h c) -> p h c", c=DH), ALU.mult, ALU.add)
                    last.then_inc(v1_ready.sem, 1)
                    for h in range(NH):
                        for t in range(NT):
                            dve.wait_ge(s_psum.sem, s_psum.nth(b, h * NT + t + 1))
                            nc.vector.tensor_reduce(negmax[:, t * NH + h:t * NH + h + 1], S[t], AX.X, ALU.max,
                                                    negate=True).then_inc(max_ready.sem, 1)
                    parts = [nm[:].rearrange("p t (h c) -> p (t h) c", c=HALF)[:, :, 48 + i] for i in range(3)]
                    dve.wait_ge(max_ready.sem, max_ready.nth(b))
                    nc.vector.tensor_scalar(nmf[:], negmax[:], 1.0 / MAXSCALE, None, ALU.mult).then_inc(nm_step.sem, 1)
                    dve.wait_ge(nm_step.sem, nm_step.nth(b, 1))
                    nc.vector.tensor_copy(parts[0], nmf[:]).then_inc(nm_step.sem, 1)
                    dve.wait_ge(nm_step.sem, nm_step.nth(b, 2))
                    nc.vector.tensor_tensor(nmr[:], nmf[:], parts[0], ALU.subtract).then_inc(nm_step.sem, 1)
                    dve.wait_ge(nm_step.sem, nm_step.nth(b, 3))
                    nc.vector.tensor_copy(parts[1], nmr[:]).then_inc(nm_step.sem, 1)
                    dve.wait_ge(nm_step.sem, nm_step.nth(b, 4))
                    nc.vector.tensor_tensor(parts[2], nmr[:], parts[1], ALU.subtract).then_inc(nm_step.sem, 1)
                    for g in range(NG):
                        dve.wait_ge(nmT_psum.sem, nmT_psum.nth(b, g + 1))
                        nc.vector.tensor_tensor(stacks[:, g, :], W[g % 2], stacks[:, g, :], ALU.add).then_inc(shifted1.sem, 1)
                    dve.wait_ge(pv_done.sem, pv_done.nth(b))
                    ctx4 = W3[:, :, 0:NH * VW].rearrange("p t (h c) -> p t h c", c=VW)
                    nc.vector.reciprocal(csum[:], ctx4[:, :, :, DH]).then_inc(csum_ready.sem, 1)
                    dve.wait_ge(csum_ready.sem, csum_ready.nth(b))
                    for t in range(NT):
                        last = nc.vector.tensor_tensor(cx[:, t, :].rearrange("p (h c) -> p h c", c=DH), ctx4[:, t, :, 0:DH],
                                                       csum[:, t, :].unsqueeze(2).broadcast_to([P, NH, DH]), ALU.mult)
                    last.then_inc(cx_ready.sem, 1)
                    dve.wait_ge(cxT_psum.sem, cxT_psum.nth(b, 2))
                    nc.vector.tensor_copy(hnT_b[:], F[1][0:HALF, 0:N]).then_inc(cxTb_ready.sem, 1)
                    dve.wait_ge(wo1_psum.sem, wo1_psum.nth(b))
                    nc.vector.tensor_tensor(h4[:], F3[:, :, 0:D], hbo[:], ALU.add).then_inc(h4_ready.sem, 1)
                    dve.wait_ge(h4_ready.sem, h4_ready.nth(b))
                    for t in range(NT):
                        last = nc.vector.bn_stats(st[:, t, :], h4[:, t, :])
                    last.then_inc(ln4_stat.sem, 1)
                    dve.wait_ge(ln4_stat.sem, ln4_stat.nth(b, 1))
                    stand(dve)
                    for t in range(NT):
                        last = nc.vector.bn_aggr(mv[:, t, :], st[:, t, :])
                    last.then_inc(ln4_stat.sem, 1)
                    dve.wait_ge(ln4_rstd.sem, ln4_rstd.nth(b))
                    for t in range(NT):
                        last = nc.vector.tensor_scalar(xn[:, t, :], h4[:, t, :], mv[:, t, 0:1], rstd[:, t:t + 1],
                                                       ALU.subtract, ALU.mult)
                    last.then_inc(xn4_ready.sem, 1)
                    dve.wait_ge(x4_hi.sem, x4_hi.nth(b, 1))
                    nc.vector.tensor_tensor(xa_lo[:], F[0][:, 0:N], xa_hi[:], ALU.subtract).then_inc(x4_lo.sem, 1)
                    dve.wait_ge(x4_hi.sem, x4_hi.nth(b, 2))
                    nc.vector.tensor_tensor(xb[HALF:P], F[1][0:HALF, 0:N], xb[0:HALF], ALU.subtract).then_inc(x4_lo.sem, 1)
                    dve.wait_ge(out_done.sem, out_done.nth(b))
                    dve.wait_ge(out_stored.sem, out_stored.before(b))
                    nc.vector.tensor_tensor(ho[:], W3[:, :, 0:D], h4[:], ALU.add).then_inc(ho_ready.sem, 1)


def kernel(x, L0_attn_Wq, L0_attn_Wk, L0_attn_Wv, L0_attn_Wf, L0_attn_bf, L0_attn_Wo, L0_attn_gamma, L0_attn_beta,
           L0_ffn_router_w, L0_ffn_w_gate, L0_ffn_w_up, L0_ffn_w_down, L0_ffn_ws_gate, L0_ffn_ws_up, L0_ffn_ws_down,
           L0_ffn_sg_w, L0_ffn_sg_b, L1_attn_Wq, L1_attn_bq, L1_attn_Wk, L1_attn_bk, L1_attn_Wv, L1_attn_bv,
           L1_attn_Wo, L1_attn_bo, L1_ffn_in_weight, L1_ffn_in_bias, L1_ffn_out_weight):
    import numpy as np
    import concourse.bacc as bacc
    from concourse.bass_utils import run_bass_kernel_spmd

    def f(a):
        return np.asarray(a)

    def rows(w):
        w = f(w)
        return np.ascontiguousarray(w[0:P]), np.concatenate([w[P:D], w[P:D]], axis=0)

    gate = f(L0_ffn_w_gate).transpose(1, 0, 2).reshape(D, E0 * D)
    up = f(L0_ffn_w_up).transpose(1, 0, 2).reshape(D, E0 * D)
    gate = np.concatenate([gate, f(L0_ffn_ws_gate)], axis=1)
    up = np.concatenate([up, f(L0_ffn_ws_up)], axis=1)
    cols = [f(L0_attn_Wq), f(L0_attn_Wk), f(L0_attn_Wf), f(L0_attn_Wf), f(L0_attn_Wv), f(L0_ffn_router_w),
            f(L0_ffn_sg_w), np.zeros((D, RW - E0 - 1), np.float32)]
    for i in range(HT0):
        cols += [gate[:, i * P:(i + 1) * P], up[:, i * P:(i + 1) * P]]
    cols.append(f(L1_ffn_in_weight).T)
    w_a, w_b = rows(np.concatenate(cols, axis=1))

    def stack(w):
        w = f(w).reshape(w.shape[0], NH, 1, DH)
        return np.concatenate([w, w, w, np.zeros_like(w)], axis=2).reshape(w.shape[0], NH * HALF)

    wq_a, wq_b = rows(np.concatenate([stack(L1_attn_Wq), stack(L1_attn_Wk), f(L1_attn_Wv)], axis=1))

    def tiles(w):
        return np.ascontiguousarray(f(w).reshape(-1, P, D).transpose(1, 0, 2))

    w_down0 = tiles(np.concatenate([f(L0_ffn_w_down).reshape(E0 * D, D), f(L0_ffn_ws_down)], axis=0))
    w_out1 = tiles(L1_ffn_out_weight)
    w_o = np.zeros((P, 4, D), np.float32)
    for i, w in enumerate((f(L0_attn_Wo), f(L1_attn_Wo))):
        w_o[:, 2 * i] = w[0:P]
        w_o[0:HALF, 2 * i + 1] = w[P:D]

    r = np.arange(P)
    consts = np.zeros((P, KCOLS), np.float32)
    consts[:, K_ID:K_ID + P] = np.eye(P)
    consts[:, K_MASK:K_MASK + P] = r[None, :] >= r[:, None]
    consts[:, K_SGN] = np.where(r < M0, -1, 1)
    consts[:, K_TERMQ] = np.where(r % HALF < DH, -1, 0)
    consts[:, K_TERMK] = np.where((r % HALF >= DH) & (r % HALF < 2 * DH), -1, 0)
    consts[:, K_QSC] = 127 * BITS
    consts[:, K_IOTA:K_IOTA + E0] = np.arange(E0)

    params = np.zeros((P, VCOLS), np.float32)
    params[:, V_BF] = np.concatenate([f(L0_attn_bf), f(L0_attn_bf)])
    params[:, V_GA], params[0:HALF, V_GB] = f(L0_attn_gamma)[0:P], f(L0_attn_gamma)[P:D]
    params[:, V_BA], params[0:HALF, V_BB] = f(L0_attn_beta)[0:P], f(L0_attn_beta)[P:D]
    params[:, V_SG] = f(L0_ffn_sg_b)[0]
    params[:, V_IN:V_IN + HT1] = f(L1_ffn_in_bias).reshape(HT1, P).T
    params[:, V_BQ:V_BQ + NG] = stack(f(L1_attn_bq)[None]).reshape(NG, P).T
    params[:, V_BK:V_BK + NG] = stack(f(L1_attn_bk)[None]).reshape(NG, P).T
    for i in range(3):
        params[48 + i::HALF, V_BK:V_BK + NG] = MAXSCALE
    params[:, V_BV:V_BV + D] = f(L1_attn_bv)[None]
    params[:, V_BO:V_BO + D] = f(L1_attn_bo)[None]

    sel = np.zeros((32, NGATE, P), np.float32)
    for i in range(NGATE):
        which = (i * P + r) // D if i < RT0 else np.full(P, E0)
        for part in range(3):
            sel[part * 9 + which, i, r] = 1

    nc = bacc.Bacc("TRN2", target_bir_lowering=False, num_devices=1)
    x = f(x)
    arrays, args = {}, []
    for name, a in (("x", x), ("w_a", w_a), ("w_b", w_b), ("wq_a", wq_a), ("wq_b", wq_b), ("w_down0", w_down0),
                    ("w_out1", w_out1), ("w_o", w_o), ("consts", consts), ("params", params), ("sel", sel)):
        arrays[name] = np.ascontiguousarray(a)
        args.append(nc.dram_tensor(name, a.shape, mybir.dt.from_np(a.dtype), kind="ExternalInput").ap())
    args.append(nc.dram_tensor("out", (x.shape[0], N, D), F32, kind="ExternalOutput").ap())
    tower(nc, *args)
    r = run_bass_kernel_spmd(nc, [arrays], core_ids=[0])
    return r.results[0]["out"]
```

```python
from contextlib import ExitStack

import concourse.bass as bass
from concourse import mybir

ALU = mybir.AluOpType
ACT = mybir.ActivationFunctionType
AX = mybir.AxisListType
F32 = mybir.dt.float32
F16 = mybir.dt.float16
BF16 = mybir.dt.bfloat16
I32 = mybir.dt.int32
U32 = mybir.dt.uint32
EXP_LN = "natural_log_exp_and_others"
GELU = "gelu_and_others"
RMAX = bass.bass_isa.ReduceOp.max

P = 128
HALF = 64
NT = 3
N = NT * P
D = 192
M0 = 64
E0 = 8
HT0 = (E0 * D + 768) // P
RT0 = E0 * D // P
NGATE = RT0 + 1
HT1 = 768 // P
NH = 12
DH = D // NH
NG = NH // 2
CH4 = HALF // DH
QUANT_HEAD = 2
STACK_LAG = 3
HID_LAG = 4
DOWN_LAG = 6
GU_RING = 6
GATE_ROWS = 1
GATE_TILES = {2: (0, 3), 3: (3, 6), 4: (6, 9), 5: (9, NGATE)}
SEG_TRANSPOSES, SEG_SCORES, SEG_WEIGHTS, SEG_OUTPUT, NORM_0 = 4, 5, 6, 7, 8
TRANSPOSES_0, DECAYS, VALUES, LIN_SCORES, LIN_OUTPUT, NORM_1 = 9, 10, 11, 12, 13, 14
TRANSPOSES_1, PROJECT, NORM_2, TRANSPOSES_2, SPLIT_2, ROUTE = 15, 16, 17, 19, 19, 21
LOG2E = 1.4426950408889634
BITS = float(1 << 23)
ROUND = 1.5 * BITS
MAXSCALE = 64.0

C_QK = 0
C_F = C_QK + 2 * M0
C_V = C_F + 2 * M0
C_R = C_V + D
RW = 16
C_GU = C_R + RW
C_IN = C_GU + HT0 * 2 * P
WCOLS = C_IN + HT1 * P
C_KS = NG * P
C_V1 = 2 * NG * P
QCOLS = C_V1 + D

K_ID, K_MASK, K_SGN, K_TERMQ, K_TERMK, K_QSC, K_IOTA = 0, 128, 256, 257, 258, 259, 260
KCOLS = K_IOTA + E0
V_BF, V_GA, V_BA, V_GB, V_BB, V_SG, V_IN, V_BQ, V_BK, V_BV, V_BO = 0, 1, 2, 3, 4, 5, 6, 12, 18, 24, 216
VCOLS = V_BO + D


class Signal:

    def __init__(self, sem, per_batch, base=0):
        self.sem, self.per_batch, self.base = sem, per_batch, base

    def nth(self, b, k=None):
        return b * self.per_batch + (self.base + self.per_batch if k is None else self.base + k)

    def before(self, b):
        assert self.base > 0
        return b * self.per_batch + self.base


def tower(nc, x, w_a, w_b, wq_a, wq_b, w_down0, w_out1, w_o, consts, params, sel, out):
    B, S, _ = x.shape
    LAST = (S - 4 * P + 1) // 2
    h3_dram = nc.dram_tensor("h3_scratch", (B, P, NT, D), F32).ap()

    ctx = ExitStack()
    with ctx:
        def sb(name, shape, dt=F32):
            return ctx.enter_context(nc.sbuf_tensor(name, shape, dt))

        based = []

        def sig(name, per_batch=1, base=0):
            made = Signal(ctx.enter_context(nc.semaphore(name)), per_batch, base)
            if base:
                based.append(made)
            return made

        passed = ctx.enter_context(nc.semaphore("passed"))

        def stand(eng):
            eng.sem_inc(passed, 1)

        wa_hi, wa_lo, wb_hi = (sb(n, [P, WCOLS], F16) for n in ("wa_hi", "wa_lo", "wb_hi"))
        wb_lo = sb("wb_lo", [HALF, WCOLS], F16)
        qa_hi, qa_lo, qb_hl = (sb(n, [P, QCOLS], F16) for n in ("qa_hi", "qa_lo", "qb_hl"))
        wdown0 = sb("wdown0", [P, HT0, D])
        wout1 = sb("wout1", [P, HT1, D])
        wo = sb("wo", [P, 4, D])
        cst = sb("cst", [P, KCOLS])
        par = sb("par", [P, VCOLS])
        selb = sb("selb", [32, NGATE, P], BF16)
        self32 = sb("self32", [32, NGATE, P])
        neg_bf = sb("neg_bf", [P, 1])
        neg_sg = sb("neg_sg", [P, 1])
        id16 = sb("id16", [P, P], F16)
        idb = sb("idb", [P, P], BF16)
        ones = sb("ones", [P, N])
        neghalf = sb("neghalf", [P, NT])
        ident = cst[:, K_ID:K_ID + P]
        mask = cst[:, K_MASK:K_MASK + P]

        xin = sb("xin", [P, NT, D])
        xs = sb("xs", [P, NT, D])
        xsT_a = sb("xsT_a", [P, N])
        xsT_b = sb("xsT_b", [HALF, N])
        prob = sb("prob", [P, NT, P])
        probT = sb("probT", [P, NT, P])
        rowmax = sb("rowmax", [P, NT])
        rowsum = sb("rowsum", [P, NT])
        rowinv = sb("rowinv", [P, NT])
        h1 = sb("h1", [P, NT, D])
        h2 = sb("h2", [P, NT, D])
        h3 = sb("h3", [P, NT, D])
        st = sb("st", [P, NT, 6])
        mv = sb("mv", [P, NT, 2])
        var_eps = sb("var_eps", [P, NT])
        rstd = sb("rstd", [P, NT])
        xn = sb("xn", [P, NT, D])
        attn_x = [sb(n, [P, N], F16)[:] for n in ("attn_xa_hi", "attn_xa_lo", "attn_xb")]
        ffn_x = [sb(n, [P, N], F16)[:] for n in ("ffn_xa_hi", "ffn_xa_lo", "ffn_xb")]
        forget = sb("forget", [P, N])
        decay = sb("decay", [P, N])
        qk_min = sb("qk_min", [P, N])
        qk = sb("qk", [P, N])
        qd = sb("qd", [M0, N])
        kd = sb("kd", [M0, N])
        vals = sb("vals", [P, NT, D + 1])
        att = sb("att", [P, NT, N])
        den = sb("den", [P, NT])
        deninv = sb("deninv", [P, NT])
        hn = sb("hn", [P, NT, D])
        hnT_a = sb("hnT_a", [P, N])
        hnT_b = sb("hnT_b", [HALF, N])
        logit = sb("logit", [P, NT, E0])
        top = sb("top", [P, NT, 8])
        top_i = sb("top_i", [P, NT, 8], U32)
        top_f = sb("top_f", [P, NT, 2])
        gexp = sb("gexp", [P, NT, 2])
        gden = sb("gden", [P, NT, 2])
        grec = sb("grec", [P, NT, 2])
        gw2 = sb("gw2", [P, NT, 2])
        hot = sb("hot", [P, NT, 2, E0])
        gate9 = sb("gate9", [P, NT, 9])
        gres = sb("gres", [P, NT, 9])
        gsplit = sb("gsplit", [P, NT, 32], BF16)
        gateT = sb("gateT", [32, N], BF16)
        gates = sb("gates", [P, NGATE, N])
        silu = sb("silu", [P, 2, N])
        gu = sb("gu", [P, GU_RING, N])
        hid = sb("hid", [P, 3, N])
        h2_kept = sb("h2_kept", [P, NT, D])
        st3 = sb("st3", [P, NT, 6])
        mv3 = sb("mv3", [P, NT, 2])
        var3 = sb("var3", [P, NT])
        inv3 = sb("inv3", [P, NT])
        xn3 = sb("xn3", [P, NT, D])
        absmax = sb("absmax", [P, 2])
        stat3 = sb("stat3", [P, B * NT, 2])
        rstd3 = sb("rstd3", [P, B * NT])
        allmax = sb("allmax", [P, 1])
        qscale = sb("qscale", [P, 1])
        qinv = sb("qinv", [P, 1])
        qnat = sb("qnat", [P, NT, D], F16)
        qT_a = sb("qT_a", [P, N], F16)
        qT_b = sb("qT_b", [P, N], F16)
        sfull = silu
        shi = sb("shi", [P, 2, N], F16)
        stacks = [sb("stacks", [P, 2 * NG, N], F16)[:],
                  gu[:].rearrange("p a n -> p (a n)").bitcast(F16).rearrange("p (a n) -> p a n", n=N)]
        v1 = [[gates[:].rearrange("p a n -> p (a n)")[:, t * NH * P:(t + 1) * NH * P] for t in range(NT)],
              [w[:, 0:2 * NH * P].bitcast(F32) for w in (wa_hi, wa_lo, wb_hi)]]

        def stack_at(j):
            return j // 2 + NG * (j % 2)

        negmax = sb("negmax", [P, NT * NH])
        nmf = sb("nmf", [P, NT * NH])
        nmr = sb("nmr", [P, NT * NH])
        mvq = sb("mvq", [P, NT, 2])
        rstdq = sb("rstdq", [P, NT])
        qx = xn3
        nm = sb("nm", [P, NT, NH * HALF], F16)
        csum = forget
        pT = [w[:, at:at + 2 * N].bitcast(I32) for w in (wa_hi, wa_lo, wb_hi)
              for at in (2 * NH * P, 2 * NH * P + 2 * N)]

        hbo = h2
        h4 = [sb("h4", [P, NT, D]), xs]
        ho = sb("ho", [P, NT, D])

        ps = ctx.enter_context(nc.psum_tensor("ps", [P, 8, 512], F32))
        F = [ps[:, 0, :], ps[:, 1, :]]
        F3 = ps[:, 0:2, :].rearrange("p a (c n) -> p (a c) n", n=256)[:, 0:NT, :]
        G = [ps[:, 2, :], ps[:, 3, :]]
        U = [ps[:, 4, :], ps[:, 5, :]]
        D3 = ps[:, 6:8, :].rearrange("p a (c n) -> p (a c) n", n=256)[:, 0:NT, :]

        def f16_bank(i):
            return ps[:, i, :].bitcast(F16)

        def cols(t, k=1):
            return slice(t * P, (t + k) * P)

        def split_terms(act, c, m):
            s = slice(c, c + m)
            return [(act[0], wa_hi[:, s]), (act[0], wa_lo[:, s]), (act[1], wa_hi[:, s]),
                    (act[2], wb_hi[:, s]), (act[2][0:HALF], wb_lo[:, s])]

        def weights_stationary(out_, act, c, m):
            terms = split_terms(act, c, m)
            for i, (a, w) in enumerate(terms):
                last = nc.tensor.matmul(out_, w, a, start=i == 0, stop=i == len(terms) - 1)
            return last

        def tokens_stationary(out_, act, c, m, t, first=True):
            terms = split_terms(act, c, m)
            for i, (a, w) in enumerate(terms):
                last = nc.tensor.matmul(out_, a[:, cols(t)], w, start=i == 0, stop=i == len(terms) - 1)
            return last

        CH = 1168
        whole, upper, lower = slice(0, P), slice(0, HALF), slice(HALF, P)
        chunks = []
        for c in range(0, WCOLS, CH):
            s = slice(c, min(c + CH, WCOLS))
            chunks.append([(w_a[:, s], wa_hi[:, s], wa_lo[:, s], whole), (w_b[:, s], wb_hi[:, s], wb_lo[:, s], upper)])
        for c in range(0, QCOLS, CH):
            s = slice(c, min(c + CH, QCOLS))
            chunks.append([(wq_a[:, s], qa_hi[:, s], qa_lo[:, s], whole), (wq_b[:, s], qb_hl[:, s], qb_hl[lower, s], lower)])
        stage = gates[:].rearrange("p a n -> p (a n)")

        def staged(n, k):
            at = ((n % 2) * 2 + k) * CH
            return stage[:, at:at + chunks[n][k][1].shape[1]]

        s_const = sig("const_landed", 4 * 16)
        s_weights = sig("weights_landed", 2 * 16)
        s_stage = [sig("staged_even", 32), sig("staged_odd", 32)]
        s_hi = sig("weights_hi", 2)
        s_lo = sig("weights_lo", 2)
        s_prep = sig("prepared", 6)
        s_mem = sig("cleared", 7)

        with nc.Block() as block:
            @block.sync
            def _(sp):
                sp.dma_start(cst[:], consts).then_inc(s_const.sem, 16)
                sp.dma_start(par[:], params).then_inc(s_const.sem, 16)
                sp.dma_start(self32[:], sel).then_inc(s_const.sem, 16)
                sp.dma_start(wo[:], w_o).then_inc(s_const.sem, 16)
                sp.wait_ge(s_const.sem, s_const.nth(0))

            @block.vector
            def _(dve):
                dve.wait_ge(s_const.sem, s_const.nth(0))
                nc.vector.tensor_copy(id16[:], ident).then_inc(s_prep.sem, 1)
                nc.vector.tensor_copy(idb[:], ident).then_inc(s_prep.sem, 1)
                nc.vector.tensor_copy(selb[:], self32[:]).then_inc(s_prep.sem, 1)
                nc.vector.tensor_scalar(neg_bf[:], par[:, V_BF:V_BF + 1], -1.0, None, ALU.mult).then_inc(s_prep.sem, 1)
                nc.vector.tensor_scalar(neg_sg[:], par[:, V_SG:V_SG + 1], -1.0, None, ALU.mult).then_inc(s_prep.sem, 1)
                nc.vector.memset(absmax[:], 0.0).then_inc(s_prep.sem, 1)

            @block.gpsimd
            def _(pool):
                nc.gpsimd.memset(xin[:], 0.0).then_inc(s_mem.sem, 1)
                nc.gpsimd.memset(ones[:], 1.0).then_inc(s_mem.sem, 1)
                nc.gpsimd.memset(neghalf[:], -0.5).then_inc(s_mem.sem, 1)
                nc.gpsimd.memset(prob[:], 0.0).then_inc(s_mem.sem, 1)
                nc.gpsimd.memset(vals[:, :, D:D + 1], 1.0).then_inc(s_mem.sem, 1)
                nc.gpsimd.memset(gsplit[:], 0.0).then_inc(s_mem.sem, 1)
                nc.gpsimd.memset(nm[:], 0.0).then_inc(s_mem.sem, 1)

        x_landed = sig("x_landed", 32)
        xs_ready = sig("xs_ready", base=1)
        xsT_psum = sig("xsT_psum", 2)
        xsTa_ready = sig("xsTa_ready")
        xsTb_ready = sig("xsTb_ready")
        scores0 = sig("scores0")
        max0 = sig("max0", 2)
        shifted0 = sig("shifted0", 2)
        exp0 = sig("exp0", 2)
        sum0 = sig("sum0", 3)
        probT_psum = sig("probT_psum")
        probT_ready = sig("probT_ready")
        tok_psum = sig("tok_psum", base=1)
        h1_ready = sig("h1_ready")
        ln_stat = sig("ln_stat", 3 * 2)
        ln_eps = sig("ln_eps", 3)
        ln_rstd = sig("ln_rstd", 3)
        xn_ready = sig("xn_ready", 3)
        xnT_psum = sig("xnT_psum", 3 * 2)
        x_hi = sig("x_hi", 2 * 2)
        x_lo = sig("x_lo", 2 * 2)
        qk_psum = sig("qk_psum")
        f_psum = sig("f_psum")
        fexp = sig("fexp")
        fcap = sig("fcap")
        flog = sig("flog")
        fcum = sig("fcum", 2)
        decay_ready = sig("decay_ready")
        qkmin_ready = sig("qkmin_ready")
        qkexp = sig("qkexp")
        qk_ready = sig("qk_ready")
        decayed = sig("decayed", 2)
        v_psum = sig("v_psum")
        v_ready = sig("v_ready")
        att_psum = sig("att_psum")
        att_diag = sig("att_diag", NT)
        att_off = sig("att_off", 2)
        num_psum = sig("num_psum")
        den_ready = sig("den_ready", 2)
        hn_ready = sig("hn_ready")
        hnTa_ready = sig("hnTa_ready")
        hnTb_ready = sig("hnTb_ready")
        wo_psum = sig("wo_psum")
        h2_ready = sig("h2_ready")
        h2_copied = sig("h2_copied", base=1)
        route_psum = sig("route_psum")
        logit_ready = sig("logit_ready", 2)
        top_ready = sig("top_ready", NT)
        topi_ready = sig("topi_ready", NT)
        topf_ready = sig("topf_ready", 2)
        gexp_ready = sig("gexp_ready", 2)
        gate_step = sig("gate_step", 11)
        gateT_psum = sig("gateT_psum")
        gateT_ready = sig("gateT_ready")
        bcast_psum = sig("bcast_psum", NGATE)
        gate_ready = sig("gate_ready", NGATE, base=1)
        g_psum = sig("g_psum", HT0)
        u_psum = sig("u_psum", HT0)
        silu_ready = sig("silu_ready", HT0, base=1)
        gu_ready = sig("gu_ready", HT0, base=1)
        hid_ready = sig("hid_ready", HT0, base=1)
        down_done = sig("down_done", HT0, base=1)
        h3_ready = sig("h3_ready", base=1)
        ln3_stat = sig("ln3_stat", 2)
        ln3_eps = sig("ln3_eps")
        ln3_rstd = sig("ln3_rstd")
        absmax_step = sig("absmax_step", 3)
        stat_kept = sig("stat_kept", 2, base=1)
        h3_stored = sig("h3_stored", 16, base=16)

        with nc.Block() as block:
            @block.sync
            def _(sp):
                for made in based:
                    sp.sem_inc(made.sem, made.base)
                based.clear()

        GT = [ps[:, 6, :], ps[:, 7, :]]

        with nc.Block() as block:
            @block.sync
            def _(sp):
                def load_x(b):
                    sp.wait_ge(xs_ready.sem, xs_ready.before(b))
                    even = x[b, 0:4 * P:2, :].rearrange("(t p) d -> p t d", p=P)
                    sp.dma_start(xin[:, 0:2, :], even).then_inc(x_landed.sem, 16)
                    sp.dma_start(xin[0:LAST, 2, :], x[b, 4 * P:S:2, :]).then_inc(x_landed.sem, 16)

                def store_h3(b):
                    sp.wait_ge(h3_ready.sem, h3_ready.nth(b))
                    sp.dma_start(h3_dram[b], h3[:]).then_inc(h3_stored.sem, 16)

                load_x(0)
                load_x(1)
                for n, halves in enumerate(chunks):
                    if n >= 2:
                        sp.wait_ge(s_hi.sem, s_hi.nth(n - 2))
                        sp.wait_ge(s_lo.sem, s_lo.nth(n - 2))
                    for k, (src, _, _, _) in enumerate(halves):
                        sp.dma_start(staged(n, k), src).then_inc(s_stage[n % 2].sem, 16)
                    if n == 3:
                        sp.dma_start(wdown0[:], w_down0).then_inc(s_weights.sem, 16)
                        sp.dma_start(wout1[:], w_out1).then_inc(s_weights.sem, 16)
                with sp.Fori(0, B - 2) as b:
                    load_x(b + 2)
                    store_h3(b)
                store_h3(B - 2)
                store_h3(B - 1)
                sp.wait_ge(h3_stored.sem, h3_stored.nth(B - 1))

            @block.gpsimd
            def _(pool):
                def copy_x(b):
                    pool.wait_ge(x_landed.sem, x_landed.nth(b))
                    pool.wait_ge(tok_psum.sem, tok_psum.before(b))
                    stand(pool)
                    nc.gpsimd.tensor_copy(xs[:], xin[:]).then_inc(xs_ready.sem, 1)

                def front_rstd(b):
                    for n in range(3):
                        pool.wait_ge(ln_stat.sem, ln_stat.nth(b, 2 * n + 2))
                        stand(pool)
                        nc.gpsimd.tensor_scalar(var_eps[:], mv[:, :, 1], 1e-5, None, ALU.add).then_inc(ln_eps.sem, 1)
                        pool.wait_ge(ln_eps.sem, ln_eps.nth(b, n + 1))
                        nc.gpsimd.tensor_tensor(rstd[:], var_eps[:], neghalf[:], ALU.pow).then_inc(ln_rstd.sem, 1)

                def keep_h2(b):
                    pool.wait_ge(h2_ready.sem, h2_ready.nth(b))
                    pool.wait_ge(h3_ready.sem, h3_ready.before(b))
                    stand(pool)
                    nc.gpsimd.tensor_copy(h2_kept[:], h2[:]).then_inc(h2_copied.sem, 1)

                def last_norm(b):
                    pool.wait_ge(ln3_stat.sem, ln3_stat.nth(b))
                    stand(pool)
                    nc.gpsimd.tensor_scalar(var3[:], mv3[:, :, 1], 1e-5, None, ALU.add).then_inc(ln3_eps.sem, 1)
                    pool.wait_ge(ln3_eps.sem, ln3_eps.nth(b))
                    nc.gpsimd.tensor_tensor(inv3[:], var3[:], neghalf[:], ALU.pow).then_inc(ln3_rstd.sem, 1)
                    pool.wait_ge(ln3_rstd.sem, ln3_rstd.nth(b))
                    stand(pool)
                    nc.gpsimd.tensor_copy(stat3[:, bass.ds(b * NT, NT), :], mv3[:]).then_inc(stat_kept.sem, 1)
                    nc.gpsimd.tensor_copy(rstd3[:, bass.ds(b * NT, NT)], inv3[:]).then_inc(stat_kept.sem, 1)

                copy_x(0)
                front_rstd(0)
                copy_x(1)
                keep_h2(0)
                front_rstd(1)
                with pool.Fori(1, B - 1) as b:
                    copy_x(b + 1)
                    keep_h2(b)
                    last_norm(b - 1)
                    front_rstd(b + 1)
                keep_h2(B - 1)
                last_norm(B - 2)
                last_norm(B - 1)

            @block.tensor
            def _(pe):
                def transposes(src, done):
                    for t in range(NT):
                        last = nc.tensor.transpose(F[0][:, cols(t)], src[:, t, 0:P], ident)
                    last.then_inc(done.sem, 1)
                    for t in range(NT):
                        last = nc.tensor.transpose(F[1][0:HALF, cols(t)], src[:, t, P:D], ident)
                    last.then_inc(done.sem, 1)

                def segment_transposes(b):
                    pe.wait_ge(xs_ready.sem, xs_ready.nth(b))
                    transposes(xs, xsT_psum)

                def segment_scores(b):
                    pe.wait_ge(xsTa_ready.sem, xsTa_ready.nth(b))
                    pe.wait_ge(xsTb_ready.sem, xsTb_ready.nth(b))
                    for t in range(NT):
                        nc.tensor.matmul(F[0][:, cols(t)], xsT_a[:, cols(t)], xsT_a[:, cols(t)], start=True, stop=False)
                        last = nc.tensor.matmul(F[0][:, cols(t)], xsT_b[:, cols(t)], xsT_b[:, cols(t)], start=False, stop=True)
                    last.then_inc(scores0.sem, 1)

                def segment_weights_transposed(b):
                    pe.wait_ge(exp0.sem, exp0.nth(b))
                    for t in range(NT):
                        last = nc.tensor.transpose(F[1][:, cols(t)], prob[:, t, :], ident)
                    last.then_inc(probT_psum.sem, 1)

                def segment_output(b):
                    pe.wait_ge(probT_ready.sem, probT_ready.nth(b))
                    for t in range(NT):
                        last = nc.tensor.matmul(F3[:, t, 0:D], probT[:, t, :], xs[:, t, :], start=True, stop=True)
                    last.then_inc(tok_psum.sem, 1)

                def norm_transposes(b, n):
                    pe.wait_ge(xn_ready.sem, xn_ready.nth(b, n + 1))
                    transposes(xn, xnT_psum)

                def forget_and_qk(b):
                    pe.wait_ge(x_hi.sem, x_hi.nth(b, 2))
                    pe.wait_ge(x_lo.sem, x_lo.nth(b, 2))
                    weights_stationary(F[1][:, 0:N], attn_x, C_F, P).then_inc(f_psum.sem, 1)
                    weights_stationary(F[0][:, 0:N], attn_x, C_QK, P).then_inc(qk_psum.sem, 1)

                def values(b):
                    pe.wait_ge(fexp.sem, fexp.nth(b))
                    pe.wait_ge(qk_ready.sem, qk_ready.nth(b))
                    for t in range(NT):
                        last = tokens_stationary(F3[:, t, 0:D], attn_x, C_V, D, t)
                    last.then_inc(v_psum.sem, 1)

                def linear_scores(b):
                    pe.wait_ge(v_ready.sem, v_ready.nth(b))
                    pe.wait_ge(decayed.sem, decayed.nth(b))
                    nc.tensor.matmul(F[0][:, 0:N], kd[:, cols(0)], qd[:], start=True, stop=True)
                    nc.tensor.matmul(F[1][:, 0:2 * P], kd[:, cols(1)], qd[:, cols(1, 2)], start=True, stop=True)
                    nc.tensor.matmul(F[1][:, 2 * P:3 * P], kd[:, cols(2)], qd[:, cols(2)],
                                     start=True, stop=True).then_inc(att_psum.sem, 1)

                def linear_output(b):
                    pe.wait_ge(att_diag.sem, att_diag.nth(b))
                    pe.wait_ge(att_off.sem, att_off.nth(b))
                    for t in range(NT):
                        for j in range(t + 1):
                            last = nc.tensor.matmul(F3[:, t, 0:D + 1], att[:, j, cols(t)], vals[:, j, :],
                                                    start=j == 0, stop=j == t)
                    last.then_inc(num_psum.sem, 1)

                def project_out(b):
                    pe.wait_ge(hnTa_ready.sem, hnTa_ready.nth(b))
                    pe.wait_ge(hnTb_ready.sem, hnTb_ready.nth(b))
                    for t in range(NT):
                        nc.tensor.matmul(F3[:, t, 0:D], hnT_a[:, cols(t)], wo[:, 0, :], start=True, stop=False)
                        last = nc.tensor.matmul(F3[:, t, 0:D], hnT_b[:, cols(t)], wo[0:HALF, 1, :],
                                                start=False, stop=True)
                    last.then_inc(wo_psum.sem, 1)

                def route(b):
                    pe.wait_ge(x_hi.sem, x_hi.nth(b))
                    pe.wait_ge(x_lo.sem, x_lo.nth(b))
                    for t in range(NT):
                        last = tokens_stationary(F[0][:, t * RW:t * RW + RW], ffn_x, C_R, RW, t)
                    last.then_inc(route_psum.sem, 1)

                def gate_rows(b):
                    pe.wait_ge(gate_step.sem, gate_step.nth(b))
                    pe.wait_ge(h3_ready.sem, h3_ready.before(b))
                    gT = GT[1].bitcast(BF16)
                    for t in range(NT):
                        last = nc.tensor.transpose(gT[0:32, cols(t)], gsplit[:, t, :], idb[:])
                    last.then_inc(gateT_psum.sem, 1)

                def gate_tiles(b, first, end):
                    if first == 0 and end > 0:
                        pe.wait_ge(gateT_ready.sem, gateT_ready.nth(b))
                    for i in range(first, end):
                        if i >= 2:
                            pe.wait_ge(gate_ready.sem, gate_ready.nth(b, i - 1))
                        nc.tensor.matmul(GT[i % 2][:, 0:N], selb[:, i, :], gateT[:],
                                         start=True, stop=True).then_inc(bcast_psum.sem, 1)

                def mixture(b, nxt):
                    for i in range(HT0 + DOWN_LAG):
                        if i < HT0:
                            c = C_GU + 2 * P * i
                            pe.wait_ge(silu_ready.sem, silu_ready.nth(b, i - 1) if i >= 2 else silu_ready.before(b))
                            weights_stationary(G[i % 2][:, 0:N], ffn_x, c, P).then_inc(g_psum.sem, 1)
                            first, end = GATE_TILES.get(i, (0, 0))
                            gate_tiles(b, first, min(first + 1, end))
                            pe.wait_ge(gu_ready.sem, gu_ready.nth(b, i - 1) if i >= 2 else gu_ready.before(b))
                            weights_stationary(U[i % 2][:, 0:N], ffn_x, c + P, P).then_inc(u_psum.sem, 1)
                        if i == GATE_ROWS:
                            gate_rows(b)
                        if i in GATE_TILES:
                            gate_tiles(b, first + 1, end)
                        j = i - DOWN_LAG
                        if j >= 0:
                            if j == 0:
                                pe.wait_ge(gate_ready.sem, gate_ready.nth(b))
                            pe.wait_ge(hid_ready.sem, hid_ready.nth(b, j + 1))
                            for t in range(NT):
                                last = nc.tensor.matmul(D3[:, t, 0:D], hid[:, j % 3, cols(t)], wdown0[:, j, :],
                                                        start=j == 0 and t != 1, stop=j == HT0 - 1,
                                                        skip_group_check=True)
                            last.then_inc(down_done.sem, 1)
                        if nxt is None:
                            continue
                        if i == SEG_TRANSPOSES:
                            segment_transposes(nxt)
                        if i == SEG_SCORES:
                            segment_scores(nxt)
                        if i == SEG_WEIGHTS:
                            segment_weights_transposed(nxt)
                        if i == SEG_OUTPUT:
                            segment_output(nxt)
                        if i == TRANSPOSES_0:
                            norm_transposes(nxt, 0)
                        if i == DECAYS:
                            forget_and_qk(nxt)
                        if i == VALUES:
                            values(nxt)
                        if i == LIN_SCORES:
                            linear_scores(nxt)
                        if i == LIN_OUTPUT:
                            linear_output(nxt)
                        if i == TRANSPOSES_1:
                            norm_transposes(nxt, 1)
                        if i == PROJECT:
                            project_out(nxt)
                        if i == TRANSPOSES_2:
                            norm_transposes(nxt, 2)
                        if i == ROUTE:
                            route(nxt)

                segment_transposes(0)
                segment_scores(0)
                segment_weights_transposed(0)
                segment_output(0)
                norm_transposes(0, 0)
                pe.wait_ge(s_lo.sem, s_lo.nth(0))
                forget_and_qk(0)
                values(0)
                linear_scores(0)
                linear_output(0)
                norm_transposes(0, 1)
                project_out(0)
                norm_transposes(0, 2)
                route(0)
                pe.wait_ge(s_lo.sem, s_lo.nth(len(chunks) - 1))
                pe.wait_ge(s_weights.sem, s_weights.nth(0))
                with pe.Fori(0, B - 1) as b:
                    mixture(b, b + 1)
                mixture(B - 1, None)

            @block.scalar
            def _(act):
                def weights_high(first, end):
                    for n in range(first, end):
                        act.wait_ge(s_stage[n % 2].sem, s_stage[n % 2].nth(n // 2))
                        for k, (_, hi, _, _) in enumerate(chunks[n]):
                            nc.scalar.activation(hi, staged(n, k), ACT.Copy).then_inc(s_hi.sem, 1)

                def copy_segments(b):
                    act.wait_ge(xsT_psum.sem, xsT_psum.nth(b, 1))
                    nc.scalar.activation(xsT_a[:], F[0][:, 0:N], ACT.Copy).then_inc(xsTa_ready.sem, 1)

                def segment_exp(b):
                    nc.scalar.preload_act_table_set(EXP_LN)
                    for s in range(2):
                        r = slice(s * HALF, (s + 1) * HALF)
                        act.wait_ge(shifted0.sem, shifted0.nth(b, s + 1))
                        nc.scalar.activation(prob[r, :, r], prob[r, :, r], ACT.Exp,
                                             scale=float(D) ** -0.5).then_inc(exp0.sem, 1)

                def copy_segment_weights(b):
                    act.wait_ge(probT_psum.sem, probT_psum.nth(b))
                    nc.scalar.activation(probT[:], F[1][:, 0:N].rearrange("p (t n) -> p t n", t=NT),
                                         ACT.Copy).then_inc(probT_ready.sem, 1)

                def split_high(b, n, dst):
                    act.wait_ge(xnT_psum.sem, xnT_psum.nth(b, 2 * n + 1))
                    nc.scalar.activation(dst[0][:], F[0][:, 0:N], ACT.Copy).then_inc(x_hi.sem, 1)
                    act.wait_ge(xnT_psum.sem, xnT_psum.nth(b, 2 * n + 2))
                    nc.scalar.activation(dst[2][0:HALF], F[1][0:HALF, 0:N], ACT.Copy).then_inc(x_hi.sem, 1)

                def decays(b):
                    nc.scalar.preload_act_table_set(EXP_LN)
                    act.wait_ge(f_psum.sem, f_psum.nth(b))
                    nc.scalar.activation(forget[:], F[1][:, 0:N], ACT.Exp, scale=-1.0,
                                         bias=neg_bf[:]).then_inc(fexp.sem, 1)
                    act.wait_ge(fcap.sem, fcap.nth(b))
                    nc.scalar.activation(forget[:], forget[:], ACT.Ln).then_inc(flog.sem, 1)
                    act.wait_ge(qkmin_ready.sem, qkmin_ready.nth(b))
                    nc.scalar.activation(qk_min[:], qk_min[:], ACT.Exp).then_inc(qkexp.sem, 1)
                    act.wait_ge(fcum.sem, fcum.nth(b))
                    nc.scalar.activation(decay[:], decay[:], ACT.Exp,
                                         scale=cst[:, K_SGN:K_SGN + 1]).then_inc(decay_ready.sem, 1)

                def copy_values(b):
                    act.wait_ge(v_psum.sem, v_psum.nth(b))
                    nc.scalar.activation(vals[:, :, 0:D], F3[:, :, 0:D], ACT.Copy).then_inc(v_ready.sem, 1)

                def copy_linear_scores(b):
                    act.wait_ge(att_diag.sem, att_diag.nth(b, 1))
                    nc.scalar.activation(att[:, 0, cols(1, 2)], F[0][:, cols(1, 2)], ACT.Copy).then_inc(att_off.sem, 1)
                    act.wait_ge(att_diag.sem, att_diag.nth(b))
                    nc.scalar.activation(att[:, 1, cols(2)], F[1][:, cols(1)], ACT.Copy).then_inc(att_off.sem, 1)

                def scale_and_shift(b):
                    act.wait_ge(xnT_psum.sem, xnT_psum.nth(b, 3))
                    nc.scalar.activation(hnT_a[:], F[0][:, 0:N], ACT.Identity, scale=par[:, V_GA:V_GA + 1],
                                         bias=par[:, V_BA:V_BA + 1]).then_inc(hnTa_ready.sem, 1)

                def gate_exp(b):
                    nc.scalar.preload_act_table_set(EXP_LN)
                    act.wait_ge(topf_ready.sem, topf_ready.nth(b))
                    nc.scalar.activation(gexp[:, :, 0], gexp[:, :, 0], ACT.Exp).then_inc(gexp_ready.sem, 1)
                    nc.scalar.activation(gexp[:, :, 1], gexp[:, :, 1], ACT.Exp, scale=-1.0,
                                         bias=neg_sg[:]).then_inc(gexp_ready.sem, 1)

                def copy_gate_rows(b):
                    act.wait_ge(gateT_psum.sem, gateT_psum.nth(b))
                    nc.scalar.activation(gateT[:], GT[1].bitcast(BF16)[0:32, 0:N], ACT.Copy).then_inc(gateT_ready.sem, 1)

                def copy_gate_tiles(b, first, end):
                    if first == 0:
                        act.wait_ge(hid_ready.sem, hid_ready.before(b))
                    for i in range(first, end):
                        act.wait_ge(bcast_psum.sem, bcast_psum.nth(b, i + 1))
                        nc.scalar.activation(gates[:, i, :], GT[i % 2][:, 0:N], ACT.Copy).then_inc(gate_ready.sem, 1)

                def mixture(b, nxt):
                    for i in range(HT0 + DOWN_LAG):
                        if i < HT0:
                            act.wait_ge(g_psum.sem, g_psum.nth(b, i + 1))
                            act.wait_ge(gu_ready.sem, gu_ready.nth(b, i - 1) if i >= 2 else gu_ready.before(b))
                            nc.scalar.activation(silu[:, i % 2, :], G[i % 2][:, 0:N], ACT.Silu).then_inc(silu_ready.sem, 1)
                        if i == GATE_ROWS:
                            copy_gate_rows(b)
                        if i in GATE_TILES:
                            copy_gate_tiles(b, *GATE_TILES[i])
                        if nxt is None:
                            continue
                        if i == SEG_TRANSPOSES:
                            copy_segments(nxt)
                        if i == SEG_SCORES:
                            segment_exp(nxt)
                        if i == SEG_WEIGHTS:
                            copy_segment_weights(nxt)
                        if i == TRANSPOSES_0:
                            split_high(nxt, 0, attn_x)
                        if i == DECAYS:
                            decays(nxt)
                        if i == VALUES:
                            copy_values(nxt)
                        if i == LIN_SCORES:
                            copy_linear_scores(nxt)
                        if i == TRANSPOSES_1:
                            scale_and_shift(nxt)
                        if i == TRANSPOSES_2:
                            split_high(nxt, 2, ffn_x)
                        if i == ROUTE:
                            gate_exp(nxt)

                copy_segments(0)
                weights_high(0, 1)
                segment_exp(0)
                copy_segment_weights(0)
                weights_high(1, 3)
                split_high(0, 0, attn_x)
                decays(0)
                weights_high(3, 4)
                copy_values(0)
                weights_high(4, 5)
                copy_linear_scores(0)
                weights_high(5, 7)
                scale_and_shift(0)
                weights_high(7, len(chunks))
                split_high(0, 2, ffn_x)
                gate_exp(0)
                with act.Fori(0, B - 1) as b:
                    mixture(b, b + 1)
                mixture(B - 1, None)

            @block.vector
            def _(dve):
                S0 = F[0][:, 0:N].rearrange("p (t n) -> p t n", t=NT)
                halves = [slice(0, HALF), slice(HALF, P)]
                iota = cst[:, K_IOTA:K_IOTA + E0].unsqueeze(1).broadcast_to([P, NT, E0])

                def weights_low(first, end):
                    for n in range(first, end):
                        for k, (_, hi, lo, rows) in enumerate(chunks[n]):
                            dve.wait_ge(s_hi.sem, s_hi.nth(n, k + 1))
                            nc.vector.tensor_tensor(lo, staged(n, k)[rows], hi[rows], ALU.subtract).then_inc(s_lo.sem, 1)

                def norm_statistics(b, n, src):
                    for t in range(NT):
                        last = nc.vector.bn_stats(st[:, t, :], src[:, t, :])
                    last.then_inc(ln_stat.sem, 1)
                    dve.wait_ge(ln_stat.sem, ln_stat.nth(b, 2 * n + 1))
                    stand(dve)
                    for t in range(NT):
                        last = nc.vector.bn_aggr(mv[:, t, :], st[:, t, :])
                    last.then_inc(ln_stat.sem, 1)

                def normalise(b, n, src):
                    dve.wait_ge(ln_rstd.sem, ln_rstd.nth(b, n + 1))
                    for t in range(NT):
                        last = nc.vector.tensor_scalar(xn[:, t, :], src[:, t, :], mv[:, t, 0:1], rstd[:, t:t + 1],
                                                       ALU.subtract, ALU.mult)
                    last.then_inc(xn_ready.sem, 1)

                def split_low(b, k, dst):
                    dve.wait_ge(x_hi.sem, x_hi.nth(b, 2 * k + 1))
                    nc.vector.tensor_tensor(dst[1][:], F[0][:, 0:N], dst[0][:], ALU.subtract).then_inc(x_lo.sem, 1)
                    dve.wait_ge(x_hi.sem, x_hi.nth(b, 2 * k + 2))
                    nc.vector.tensor_tensor(dst[2][HALF:P], F[1][0:HALF, 0:N], dst[2][0:HALF],
                                            ALU.subtract).then_inc(x_lo.sem, 1)

                def copy_segments(b):
                    dve.wait_ge(xsT_psum.sem, xsT_psum.nth(b, 2))
                    nc.vector.tensor_copy(xsT_b[:], F[1][0:HALF, 0:N]).then_inc(xsTb_ready.sem, 1)

                def segment_softmax(b):
                    dve.wait_ge(scores0.sem, scores0.nth(b))
                    for r in halves:
                        nc.vector.tensor_reduce(rowmax[r], S0[r, :, r], AX.X, ALU.max).then_inc(max0.sem, 1)
                    for s, r in enumerate(halves):
                        dve.wait_ge(max0.sem, max0.nth(b, s + 1))
                        nc.vector.tensor_tensor(prob[r, :, r], S0[r, :, r],
                                                rowmax[r].unsqueeze(2).broadcast_to([HALF, NT, HALF]),
                                                ALU.subtract).then_inc(shifted0.sem, 1)
                    for s, r in enumerate(halves):
                        dve.wait_ge(exp0.sem, exp0.nth(b, s + 1))
                        nc.vector.tensor_reduce(rowsum[r], prob[r, :, r], AX.X, ALU.add).then_inc(sum0.sem, 1)
                    dve.wait_ge(sum0.sem, sum0.nth(b, 2))
                    nc.vector.reciprocal(rowinv[:], rowsum[:]).then_inc(sum0.sem, 1)

                def segment_output(b):
                    dve.wait_ge(sum0.sem, sum0.nth(b))
                    dve.wait_ge(tok_psum.sem, tok_psum.nth(b))
                    nc.vector.tensor_tensor(h1[:], F3[:, :, 0:D], rowinv[:].unsqueeze(2).broadcast_to([P, NT, D]),
                                            ALU.mult).then_inc(h1_ready.sem, 1)
                    dve.wait_ge(h1_ready.sem, h1_ready.nth(b))
                    norm_statistics(b, 0, h1)

                def decays(b):
                    dve.wait_ge(fexp.sem, fexp.nth(b))
                    nc.vector.tensor_scalar(forget[:], forget[:], 1.0, 1e6, ALU.add, ALU.min).then_inc(fcap.sem, 1)
                    dve.wait_ge(qk_psum.sem, qk_psum.nth(b))
                    nc.vector.tensor_scalar(qk_min[:], F[0][:, 0:N], 0.0, None, ALU.min).then_inc(qkmin_ready.sem, 1)
                    dve.wait_ge(flog.sem, flog.nth(b))
                    nc.vector.tensor_tensor_scan(decay[:], ones[:], forget[:], 0.0, ALU.mult, ALU.add).then_inc(fcum.sem, 1)
                    dve.wait_ge(fcum.sem, fcum.nth(b, 1))
                    nc.vector.tensor_scalar(decay[:], decay[:], 20.0, -20.0, ALU.min, ALU.max).then_inc(fcum.sem, 1)
                    dve.wait_ge(qkexp.sem, qkexp.nth(b))
                    nc.vector.scalar_tensor_tensor(qk[:], F[0][:, 0:N], 0.0, qk_min[:], ALU.max,
                                                   ALU.add).then_inc(qk_ready.sem, 1)
                    dve.wait_ge(qk_ready.sem, qk_ready.nth(b))
                    dve.wait_ge(decay_ready.sem, decay_ready.nth(b))
                    nc.vector.scalar_tensor_tensor(qd[:], qk[0:M0], float(M0) ** -0.5, decay[0:M0], ALU.mult,
                                                   ALU.mult).then_inc(decayed.sem, 1)
                    nc.vector.tensor_tensor(kd[:], qk[M0:P], decay[M0:P], ALU.mult).then_inc(decayed.sem, 1)

                def mask_linear_scores(b):
                    dve.wait_ge(att_psum.sem, att_psum.nth(b))
                    for j in range(NT):
                        src = F[0][:, cols(0)] if j == 0 else F[1][:, cols(2 * (j - 1))]
                        nc.vector.tensor_tensor(att[:, j, cols(j)], src, mask, ALU.mult).then_inc(att_diag.sem, 1)

                def linear_output(b):
                    dve.wait_ge(num_psum.sem, num_psum.nth(b))
                    nc.vector.tensor_scalar(den[:], F3[:, :, D], 1e-6, None, ALU.add).then_inc(den_ready.sem, 1)
                    dve.wait_ge(den_ready.sem, den_ready.nth(b, 1))
                    nc.vector.reciprocal(deninv[:], den[:]).then_inc(den_ready.sem, 1)
                    dve.wait_ge(den_ready.sem, den_ready.nth(b, 2))
                    nc.vector.tensor_tensor(hn[:], F3[:, :, 0:D], deninv[:].unsqueeze(2).broadcast_to([P, NT, D]),
                                            ALU.mult).then_inc(hn_ready.sem, 1)
                    dve.wait_ge(hn_ready.sem, hn_ready.nth(b))
                    norm_statistics(b, 1, hn)

                def scale_and_shift(b):
                    dve.wait_ge(xnT_psum.sem, xnT_psum.nth(b, 4))
                    nc.vector.tensor_scalar(hnT_b[:], F[1][0:HALF, 0:N], par[0:HALF, V_GB:V_GB + 1],
                                            par[0:HALF, V_BB:V_BB + 1], ALU.mult, ALU.add).then_inc(hnTb_ready.sem, 1)

                def add_attention(b):
                    dve.wait_ge(wo_psum.sem, wo_psum.nth(b))
                    dve.wait_ge(h2_copied.sem, h2_copied.before(b))
                    nc.vector.tensor_tensor(h2[:], F3[:, :, 0:D], h1[:], ALU.add).then_inc(h2_ready.sem, 1)
                    dve.wait_ge(h2_ready.sem, h2_ready.nth(b))
                    norm_statistics(b, 2, h2)

                def top_two(b):
                    dve.wait_ge(route_psum.sem, route_psum.nth(b))
                    R = F[0][:, 0:NT * RW].rearrange("p (t n) -> p t n", t=NT)
                    nc.vector.tensor_copy(logit[:], R[:, :, 0:E0]).then_inc(logit_ready.sem, 1)
                    nc.vector.tensor_copy(gexp[:, :, 1], R[:, :, E0]).then_inc(logit_ready.sem, 1)
                    dve.wait_ge(logit_ready.sem, logit_ready.nth(b, 1))
                    stand(dve)
                    for t in range(NT):
                        nc.vector.max(top[:, t, :], logit[:, t, :]).then_inc(top_ready.sem, 1)
                    for t in range(NT):
                        dve.wait_ge(top_ready.sem, top_ready.nth(b, t + 1))
                        stand(dve)
                        nc.vector.max_index(top_i[:, t, :], top[:, t, :], logit[:, t, :]).then_inc(topi_ready.sem, 1)
                    dve.wait_ge(topi_ready.sem, topi_ready.nth(b))
                    nc.vector.tensor_tensor(gexp[:, :, 0], top[:, :, 1], top[:, :, 0], ALU.subtract).then_inc(topf_ready.sem, 1)
                    nc.vector.tensor_copy(top_f[:], top_i[:, :, 0:2]).then_inc(topf_ready.sem, 1)

                def gate_weights(b):
                    k = 0

                    def step(ins):
                        nonlocal k
                        k += 1
                        ins.then_inc(gate_step.sem, 1)
                        dve.wait_ge(gate_step.sem, gate_step.nth(b, k))

                    dve.wait_ge(gexp_ready.sem, gexp_ready.nth(b))
                    step(nc.vector.tensor_scalar(gden[:], gexp[:], 1.0, None, ALU.add))
                    step(nc.vector.reciprocal(grec[:], gden[:]))
                    nc.vector.tensor_copy(gate9[:, :, E0], grec[:, :, 1])
                    step(nc.vector.tensor_scalar(gden[:, :, 1], grec[:, :, 1], -1.0, 1.0, ALU.mult, ALU.add))
                    step(nc.vector.tensor_tensor(gw2[:, :, 0], grec[:, :, 0], gden[:, :, 1], ALU.mult))
                    nc.vector.tensor_tensor(gw2[:, :, 1], gw2[:, :, 0], gexp[:, :, 0], ALU.mult)
                    for i in range(2):
                        last = nc.vector.tensor_tensor(hot[:, :, i, :], iota,
                                                       top_f[:, :, i].unsqueeze(2).broadcast_to([P, NT, E0]), ALU.is_equal)
                    step(last)
                    for i in range(2):
                        last = nc.vector.tensor_tensor(hot[:, :, i, :], hot[:, :, i, :],
                                                       gw2[:, :, i].unsqueeze(2).broadcast_to([P, NT, E0]), ALU.mult)
                    step(last)
                    step(nc.vector.tensor_tensor(gate9[:, :, 0:E0], hot[:, :, 0, :], hot[:, :, 1, :], ALU.add))
                    step(nc.vector.tensor_copy(gsplit[:, :, 0:9], gate9[:]))
                    step(nc.vector.tensor_tensor(gres[:], gate9[:], gsplit[:, :, 0:9], ALU.subtract))
                    step(nc.vector.tensor_copy(gsplit[:, :, 9:18], gres[:]))
                    step(nc.vector.tensor_tensor(gsplit[:, :, 18:27], gres[:], gsplit[:, :, 9:18], ALU.subtract))
                    assert k == gate_step.per_batch

                def finish(b):
                    dve.wait_ge(down_done.sem, down_done.nth(b))
                    dve.wait_ge(h3_stored.sem, h3_stored.before(b))
                    dve.wait_ge(h2_copied.sem, h2_copied.nth(b))
                    nc.vector.tensor_tensor(h3[:], D3[:, :, 0:D], h2_kept[:], ALU.add).then_inc(h3_ready.sem, 1)

                def finish_statistics(b):
                    dve.wait_ge(h3_ready.sem, h3_ready.nth(b))
                    for t in range(NT):
                        last = nc.vector.bn_stats(st3[:, t, :], h3[:, t, :])
                    last.then_inc(ln3_stat.sem, 1)

                def finish_norm(b):
                    dve.wait_ge(stat_kept.sem, stat_kept.before(b))
                    dve.wait_ge(ln3_stat.sem, ln3_stat.nth(b, 1))
                    stand(dve)
                    for t in range(NT):
                        last = nc.vector.bn_aggr(mv3[:, t, :], st3[:, t, :])
                    last.then_inc(ln3_stat.sem, 1)

                def finish_absmax(b):
                    dve.wait_ge(ln3_rstd.sem, ln3_rstd.nth(b))
                    for t in range(NT):
                        last = nc.vector.tensor_scalar(xn3[:, t, :], h3[:, t, :], mv3[:, t, 0:1], inv3[:, t:t + 1],
                                                       ALU.subtract, ALU.mult)
                    last.then_inc(absmax_step.sem, 1)
                    dve.wait_ge(absmax_step.sem, absmax_step.nth(b, 1))
                    nc.vector.tensor_reduce(absmax[:, 1:2], xn3[:], AX.XY, ALU.max,
                                            apply_absolute_value=True).then_inc(absmax_step.sem, 1)
                    dve.wait_ge(absmax_step.sem, absmax_step.nth(b, 2))
                    nc.vector.tensor_tensor(absmax[:, 0:1], absmax[:, 0:1], absmax[:, 1:2],
                                            ALU.max).then_inc(absmax_step.sem, 1)

                def mixture(b, nxt, prev):
                    gate_weights(b)
                    if prev is not None:
                        finish(prev)
                    for i in range(HT0 + DOWN_LAG):
                        if i < HT0:
                            dve.wait_ge(silu_ready.sem, silu_ready.nth(b, i + 1))
                            dve.wait_ge(u_psum.sem, u_psum.nth(b, i + 1))
                            dve.wait_ge(hid_ready.sem, hid_ready.nth(b, i - GU_RING + 1) if i >= GU_RING
                                        else hid_ready.before(b))
                            nc.vector.tensor_tensor(gu[:, i % GU_RING, :], U[i % 2][:, 0:N], silu[:, i % 2, :],
                                                    ALU.mult).then_inc(gu_ready.sem, 1)
                        j = i - HID_LAG
                        if 0 <= j < HT0:
                            dve.wait_ge(gu_ready.sem, gu_ready.nth(b, j + 1))
                            dve.wait_ge(gate_ready.sem, gate_ready.nth(b, min(j, RT0) + 1))
                            dve.wait_ge(down_done.sem, down_done.nth(b, j - 2) if j >= 3 else down_done.before(b))
                            nc.vector.tensor_tensor(hid[:, j % 3, :], gu[:, j % GU_RING, :], gates[:, min(j, RT0), :],
                                                    ALU.mult).then_inc(hid_ready.sem, 1)
                        if i == 1 and prev is not None:
                            finish_statistics(prev)
                        if i == 2 and prev is not None:
                            finish_norm(prev)
                        if i == 3 and prev is not None:
                            finish_absmax(prev)
                        if nxt is None:
                            continue
                        if i == SEG_TRANSPOSES:
                            copy_segments(nxt)
                        if i == SEG_SCORES:
                            segment_softmax(nxt)
                        if i == SEG_OUTPUT:
                            segment_output(nxt)
                        if i == NORM_0:
                            normalise(nxt, 0, h1)
                        if i == TRANSPOSES_0:
                            split_low(nxt, 0, attn_x)
                        if i == DECAYS:
                            decays(nxt)
                        if i == LIN_SCORES:
                            mask_linear_scores(nxt)
                        if i == LIN_OUTPUT:
                            linear_output(nxt)
                        if i == NORM_1:
                            normalise(nxt, 1, hn)
                        if i == TRANSPOSES_1:
                            scale_and_shift(nxt)
                        if i == PROJECT:
                            add_attention(nxt)
                        if i == NORM_2:
                            normalise(nxt, 2, h2)
                        if i == SPLIT_2:
                            split_low(nxt, 1, ffn_x)
                        if i == ROUTE:
                            top_two(nxt)

                copy_segments(0)
                weights_low(0, 1)
                segment_softmax(0)
                segment_output(0)
                weights_low(1, 3)
                normalise(0, 0, h1)
                split_low(0, 0, attn_x)
                decays(0)
                weights_low(3, 5)
                mask_linear_scores(0)
                weights_low(5, 6)
                linear_output(0)
                weights_low(6, 7)
                normalise(0, 1, hn)
                scale_and_shift(0)
                weights_low(7, len(chunks))
                add_attention(0)
                normalise(0, 2, h2)
                split_low(0, 1, ffn_x)
                top_two(0)
                mixture(0, 1, None)
                with dve.Fori(1, B - 1) as b:
                    mixture(b, b + 1, b - 1)
                mixture(B - 1, None, B - 2)
                finish(B - 1)
                finish_statistics(B - 1)
                finish_norm(B - 1)
                finish_absmax(B - 1)

        S = [ps[:, 0, 0:N], ps[:, 1, 0:N]]
        T = [ps[:, 2, 0:N], ps[:, 3, 0:N]]
        Q = [ps[:, 4, 0:N], ps[:, 5, 0:N]]
        Q16 = [ps[:, 4, :].bitcast(F16), ps[:, 5, :].bitcast(F16)]
        CT = [ps[:, 6, 0:N], ps[:, 7, 0:N]]
        M = T
        V3 = ps[:, 2:4, :].rearrange("p a (c n) -> p (a c) n", n=256)[:, 0:NT, :]
        W3 = D3
        nm_parts = [nm[:].rearrange("p t (h c) -> p (t h) c", c=HALF)[:, :, 48 + i] for i in range(3)]
        allmax_ready = sig("allmax_ready")
        zeros_ready = sig("zeros_ready", 2 * NT)
        ones_ready = sig("ones_ready", 2 * NT)
        qscale_ready = sig("qscale_ready", 2)
        qx_landed = sig("qx_landed", 16)
        stat_ready = sig("stat_ready", 2)
        xq_ready = sig("xq_ready", 3, base=1)
        qnat_ready = sig("qnat_ready")
        qT_psum = sig("qT_psum", 2)
        qTa_ready = sig("qTa_ready", 2)
        qTb_ready = sig("qTb_ready")
        stack_psum = sig("stack_psum", 2 * NG)
        sfull_ready = sig("sfull_ready", 2 * NG)
        stack_ready = sig("stack_ready", 2 * NG, base=1)
        v1_psum = sig("v1_psum")
        v1_ready = sig("v1_ready", base=1)
        s_psum = sig("s_psum", NH * NT)
        max_ready = sig("max_ready", NH * NT)
        nm_step = sig("nm_step", 5)
        nmT_psum = sig("nmT_psum", NG)
        shifted1 = sig("shifted1", NG)
        sT_psum = sig("sT_psum", NH * NT)
        p_ready = sig("p_ready", NH * NT)
        pv_done = sig("pv_done", NH, base=1)
        csum_ready = sig("csum_ready", NH // CH4 * NT)
        cx_ready = sig("cx_ready", NH // CH4)
        wo1_psum = sig("wo1_psum")
        res_landed = sig("res_landed", 16)
        hbo_ready = sig("hbo_ready", base=1)
        h4_ready = sig("h4_ready", base=1)
        ln4_stat = sig("ln4_stat", 2)
        ln4_eps = sig("ln4_eps")
        ln4_rstd = sig("ln4_rstd")
        xn4_ready = sig("xn4_ready")
        xn4T_psum = sig("xn4T_psum", 2)
        x4_hi = sig("x4_hi", 2)
        x4_lo = sig("x4_lo", 2)
        in_psum = sig("in_psum", HT1)
        gelu_ready = sig("gelu_ready", HT1)
        out_done = sig("out_done", HT1, base=1)
        ho_ready = sig("ho_ready", base=1)
        out_stored = sig("out_stored", 16, base=16)

        with nc.Block() as block:
            @block.sync
            def _(sp):
                for made in based:
                    sp.sem_inc(made.sem, made.base)

        with nc.Block() as block:
            @block.sync
            def _(sp):
                def load_quant(b):
                    sp.wait_ge(xq_ready.sem, xq_ready.before(b))
                    sp.dma_start(h1[:], h3_dram[b]).then_inc(qx_landed.sem, 16)

                def store_out(b):
                    sp.wait_ge(ho_ready.sem, ho_ready.nth(b))
                    sp.dma_start(out[b].rearrange("(t p) d -> p t d", p=P), ho[:]).then_inc(out_stored.sem, 16)

                def step(b, done, has_next2):
                    if has_next2:
                        load_quant(b + 2)
                    sp.wait_ge(hbo_ready.sem, hbo_ready.before(b))
                    sp.dma_start(h3[:], h3_dram[b]).then_inc(res_landed.sem, 16)
                    if done is not None:
                        store_out(done)

                load_quant(0)
                load_quant(1)
                step(0, None, True)
                step(1, None, True)
                with sp.Fori(2, B - 2) as b:
                    step(b, b - 2, True)
                step(B - 2, B - 4, False)
                step(B - 1, B - 3, False)
                store_out(B - 2)
                store_out(B - 1)
                sp.wait_ge(out_stored.sem, out_stored.nth(B - 1))

            @block.gpsimd
            def _(pool):
                def statistics(b):
                    pool.wait_ge(xq_ready.sem, xq_ready.before(b))
                    stand(pool)
                    nc.gpsimd.tensor_copy(mvq[:], stat3[:, bass.ds(b * NT, NT), :]).then_inc(stat_ready.sem, 1)
                    nc.gpsimd.tensor_copy(rstdq[:], rstd3[:, bass.ds(b * NT, NT)]).then_inc(stat_ready.sem, 1)

                def step(b, last_q):
                    if not last_q:
                        statistics(b + 2)
                    pool.wait_ge(res_landed.sem, res_landed.nth(b))
                    pool.wait_ge(h4_ready.sem, h4_ready.before(b))
                    nc.gpsimd.tensor_tensor(hbo[:], h3[:], par[:, V_BO:V_BO + D].unsqueeze(1).broadcast_to([P, NT, D]),
                                            ALU.add).then_inc(hbo_ready.sem, 1)
                    pool.wait_ge(ln4_stat.sem, ln4_stat.nth(b))
                    stand(pool)
                    nc.gpsimd.tensor_scalar(var_eps[:], mv[:, :, 1], 1e-5, None, ALU.add).then_inc(ln4_eps.sem, 1)
                    pool.wait_ge(ln4_eps.sem, ln4_eps.nth(b))
                    nc.gpsimd.tensor_tensor(rstd[:], var_eps[:], neghalf[:], ALU.pow).then_inc(ln4_rstd.sem, 1)

                nc.gpsimd.partition_all_reduce(allmax[:], absmax[:, 0:1], P, RMAX).then_inc(allmax_ready.sem, 1)
                statistics(0)
                for par_ in range(2):
                    for t in range(NT):
                        nc.gpsimd.memset(v1[par_][t], 0.0).then_inc(zeros_ready.sem, 1)
                for par_ in range(2):
                    for t in range(NT):
                        pool.wait_ge(zeros_ready.sem, zeros_ready.nth(0, par_ * NT + t + 1))
                        nc.gpsimd.memset(v1[par_][t].rearrange("p (h c) -> p h c", c=P)[:, :, HALF:HALF + DH],
                                         1.0).then_inc(ones_ready.sem, 1)
                statistics(1)
                with pool.Fori(0, B - 2) as b:
                    step(b, False)
                step(B - 2, True)
                step(B - 1, True)

            @block.tensor
            def _(pe):
                def quant_transposes(b):
                    pe.wait_ge(qnat_ready.sem, qnat_ready.nth(b))
                    for t in range(NT):
                        last = nc.tensor.transpose(Q16[0][:, cols(t)], qnat[:, t, 0:P], id16[:])
                    last.then_inc(qT_psum.sem, 1)
                    for t in range(NT):
                        last = nc.tensor.transpose(Q16[1][0:HALF, cols(t)], qnat[:, t, P:D], id16[:])
                    last.then_inc(qT_psum.sem, 1)

                def stack(b, j):
                    if j == 0:
                        pe.wait_ge(qTa_ready.sem, qTa_ready.nth(b))
                        pe.wait_ge(qTb_ready.sem, qTb_ready.nth(b))
                    if j >= 2:
                        pe.wait_ge(sfull_ready.sem, sfull_ready.nth(b, j - 1))
                    s = slice(stack_at(j) * P, (stack_at(j) + 1) * P)
                    nc.tensor.matmul(Q[j % 2], qa_hi[:, s], qT_a[:], start=True, stop=False)
                    nc.tensor.matmul(Q[j % 2], qa_lo[:, s], qT_a[:], start=False, stop=False)
                    nc.tensor.matmul(Q[j % 2], qb_hl[:, s], qT_b[:], start=False, stop=True).then_inc(stack_psum.sem, 1)

                def values(b):
                    s = slice(C_V1, C_V1 + D)
                    for t in range(NT):
                        nc.tensor.matmul(V3[:, t, 0:D], qT_a[:, cols(t)], qa_hi[:, s], start=True, stop=False)
                        nc.tensor.matmul(V3[:, t, 0:D], qT_a[:, cols(t)], qa_lo[:, s], start=False, stop=False)
                        last = nc.tensor.matmul(V3[:, t, 0:D], qT_b[:, cols(t)], qb_hl[:, s], start=False, stop=True)
                    last.then_inc(v1_psum.sem, 1)

                def scores(b, par_, h, t, split_of=None):
                    st_ = stacks[par_]
                    r = slice((h % 2) * HALF, (h % 2 + 1) * HALF)
                    n = h * NT + t
                    if n == 0:
                        pe.wait_ge(stack_ready.sem, stack_ready.nth(b))
                    if n == 0 and split_of is not None:
                        pe.wait_ge(x4_lo.sem, x4_lo.nth(split_of))
                    if n >= 2:
                        pe.wait_ge(max_ready.sem, max_ready.nth(b, n - 1))
                    nc.tensor.matmul(S[n % 2], st_[r, h // 2, cols(t)], st_[r, NG + h // 2, :],
                                     start=True, stop=True).then_inc(s_psum.sem, 1)

                def maxima_rows(b, par_, g, values_of=None):
                    if g == 0:
                        pe.wait_ge(nm_step.sem, nm_step.nth(b))
                    if g == 0 and values_of is not None:
                        pe.wait_ge(v1_ready.sem, v1_ready.nth(values_of))
                    if g >= 2:
                        pe.wait_ge(shifted1.sem, shifted1.nth(b, g - 1))
                    for t in range(NT):
                        nc.tensor.matmul(M[g % 2][:, cols(t)], id16[:], stacks[par_][:, g, cols(t)], start=True, stop=False)
                        last = nc.tensor.matmul(M[g % 2][:, cols(t)], nm[:, t, g * P:(g + 1) * P], id16[:],
                                                start=False, stop=True)
                    last.then_inc(nmT_psum.sem, 1)

                def shifted_scores(b, par_, h, m):
                    st_ = stacks[par_]
                    r = slice((h % 2) * HALF, (h % 2 + 1) * HALF)
                    n = h * NT + m
                    if n == 0:
                        pe.wait_ge(shifted1.sem, shifted1.nth(b))
                    if n >= 2:
                        pe.wait_ge(p_ready.sem, p_ready.nth(b, n - 1))
                    nc.tensor.matmul(T[n % 2], st_[r, NG + h // 2, cols(m)], st_[r, h // 2, :],
                                     start=True, stop=True).then_inc(sT_psum.sem, 1)

                def weigh_values(b, par_, h, m, f):
                    pe.wait_ge(p_ready.sem, p_ready.nth(b, h * NT + m + 1))
                    if h == 0 and m == 0 and f is not None:
                        pe.wait_ge(ho_ready.sem, ho_ready.before(f))
                    if h == 2 * CH4 and m == 0:
                        pe.wait_ge(cx_ready.sem, cx_ready.nth(b, 1))
                    at = h * P - (h % CH4) * DH
                    last = nc.tensor.matmul(CT[(h // CH4) % 2], v1[par_][m][:, at:at + P],
                                            pT[(h % 2) * NT + m].bitcast(F32),
                                            start=h % CH4 == 0 and m == 0, stop=h % CH4 == CH4 - 1 and m == NT - 1)
                    if m == NT - 1:
                        last.then_inc(pv_done.sem, 1)

                def project_out(b):
                    pe.wait_ge(cx_ready.sem, cx_ready.nth(b))
                    for t in range(NT):
                        nc.tensor.matmul(F3[:, t, 0:D], hnT_a[:, cols(t)], wo[:, 2, :], start=True, stop=False)
                        last = nc.tensor.matmul(F3[:, t, 0:D], hnT_b[:, cols(t)], wo[0:HALF, 3, :], start=False, stop=True)
                    last.then_inc(wo1_psum.sem, 1)

                def norm_transposes(b):
                    pe.wait_ge(xn4_ready.sem, xn4_ready.nth(b))
                    for t in range(NT):
                        last = nc.tensor.transpose(F[0][:, cols(t)], xn[:, t, 0:P], ident)
                    last.then_inc(xn4T_psum.sem, 1)
                    for t in range(NT):
                        last = nc.tensor.transpose(F[1][0:HALF, cols(t)], xn[:, t, P:D], ident)
                    last.then_inc(xn4T_psum.sem, 1)

                def ffn_in(b, i, stacks_of):
                    if i == 0:
                        pe.wait_ge(x4_hi.sem, x4_hi.nth(b))
                        pe.wait_ge(x4_lo.sem, x4_lo.nth(b))
                    if i < 2 and stacks_of is not None:
                        pe.wait_ge(sfull_ready.sem, sfull_ready.nth(stacks_of, 2 * NG - 1 + i))
                    if i >= 2:
                        pe.wait_ge(gelu_ready.sem, gelu_ready.nth(b, i - 1))
                    weights_stationary(Q[i % 2], ffn_x, C_IN + i * P, P).then_inc(in_psum.sem, 1)

                def ffn_out(b, j):
                    pe.wait_ge(gelu_ready.sem, gelu_ready.nth(b, j + 1))
                    for t in range(NT):
                        last = nc.tensor.matmul(W3[:, t, 0:D], hid[:, j % 3, cols(t)], wout1[:, j, :],
                                                start=j == 0 and t != 1, stop=j == HT1 - 1,
                                                skip_group_check=True)
                    last.then_inc(out_done.sem, 1)

                def step(b, par_, f, has_next, has_next2):
                    for h in range(NH + 1):
                        for m in range(NT):
                            if h < NH:
                                shifted_scores(b, par_, h, m)
                                if has_next:
                                    scores(b + 1, 1 - par_, h, m, f)
                            if h > 0:
                                weigh_values(b, par_, h - 1, m, f)
                        if has_next2 and h == QUANT_HEAD:
                            quant_transposes(b + 2)
                        if has_next2 and STACK_LAG <= h < NH:
                            stack(b + 2, h - STACK_LAG)
                    if has_next2:
                        for j in range(NH - STACK_LAG, 2 * NG):
                            if j == 2 * NG - 1:
                                values(b + 2)
                            stack(b + 2, j)
                    if f is not None:
                        ffn_in(f, 0, b + 2 if has_next2 else None)
                        ffn_in(f, 1, b + 2 if has_next2 else None)
                    if f is not None:
                        ffn_in(f, 2, None)
                    project_out(b)
                    for i in range(3, HT1 + 3):
                        if has_next:
                            maxima_rows(b + 1, 1 - par_, i - 3, b + 2 if has_next2 else None)
                        if i == HT1 + 2:
                            norm_transposes(b)
                        if f is not None:
                            ffn_out(f, i - 3)
                            if i < HT1:
                                ffn_in(f, i, None)

                quant_transposes(0)
                for j in range(2 * NG):
                    stack(0, j)
                values(0)
                pe.wait_ge(sfull_ready.sem, sfull_ready.nth(0))
                quant_transposes(1)
                for h in range(NH):
                    for t in range(NT):
                        scores(0, 0, h, t)
                    stack(1, h)
                pe.wait_ge(v1_ready.sem, v1_ready.nth(0))
                values(1)
                for g in range(NG):
                    maxima_rows(0, 0, g, 1)
                step(0, 0, None, True, True)
                step(1, 1, 0, True, True)
                with pe.Fori(2, B - 2, 2) as b:
                    step(b, 0, b - 1, True, True)
                    step(b + 1, 1, b, True, True)
                step(B - 2, 0, B - 3, True, False)
                step(B - 1, 1, B - 2, False, False)
                for i in range(HT1 + 2):
                    if i < HT1:
                        ffn_in(B - 1, i, None)
                    if i == 2:
                        pe.wait_ge(ho_ready.sem, ho_ready.nth(B - 2))
                    if i >= 2:
                        ffn_out(B - 1, i - 2)

            @block.scalar
            def _(act):
                def copy_quant(b):
                    act.wait_ge(qT_psum.sem, qT_psum.nth(b, 1))
                    nc.scalar.activation(qT_a[:], Q16[0][:, 0:N], ACT.Copy).then_inc(qTa_ready.sem, 1)
                    act.wait_ge(qT_psum.sem, qT_psum.nth(b, 2))
                    nc.scalar.activation(qT_b[0:HALF], Q16[1][0:HALF, 0:N], ACT.Copy).then_inc(qTa_ready.sem, 1)

                def scale_stack(b, j):
                    act.wait_ge(stack_psum.sem, stack_psum.nth(b, j + 1))
                    act.wait_ge(stack_ready.sem, stack_ready.nth(b, j - 1) if j >= 2 else stack_ready.before(b))
                    v = V_BQ + stack_at(j)
                    for dst in (sfull, shi):
                        last = nc.scalar.activation(dst[:, j % 2, :], Q[j % 2], ACT.Identity, scale=qscale[:],
                                                    bias=par[:, v:v + 1])
                    last.then_inc(sfull_ready.sem, 1)

                def weights(b, h):
                    for m in range(NT):
                        n = h * NT + m
                        act.wait_ge(sT_psum.sem, sT_psum.nth(b, n + 1))
                        act.wait_ge(pv_done.sem, pv_done.nth(b, h - 1) if h >= 2 else pv_done.before(b))
                        nc.scalar.activation(pT[(h % 2) * NT + m], T[n % 2], ACT.Relu, scale=LOG2E * BITS,
                                             bias=cst[:, K_QSC:K_QSC + 1]).then_inc(p_ready.sem, 1)

                def split_high(b):
                    act.wait_ge(xn4T_psum.sem, xn4T_psum.nth(b, 1))
                    nc.scalar.activation(ffn_x[0][:], F[0][:, 0:N], ACT.Copy).then_inc(x4_hi.sem, 1)
                    act.wait_ge(xn4T_psum.sem, xn4T_psum.nth(b, 2))
                    nc.scalar.activation(ffn_x[2][0:HALF], F[1][0:HALF, 0:N], ACT.Copy).then_inc(x4_hi.sem, 1)

                def gelu(b, i):
                    act.wait_ge(in_psum.sem, in_psum.nth(b, i + 1))
                    act.wait_ge(out_done.sem, out_done.nth(b, i - 2) if i >= 3 else out_done.before(b))
                    nc.scalar.activation(hid[:, i % 3, :], Q[i % 2], ACT.Gelu,
                                         bias=par[:, V_IN + i:V_IN + i + 1]).then_inc(gelu_ready.sem, 1)

                def shift(b, par_, g):
                    act.wait_ge(nmT_psum.sem, nmT_psum.nth(b, g + 1))
                    nc.scalar.activation(stacks[par_][:, g, :], M[g % 2], ACT.Copy).then_inc(shifted1.sem, 1)

                def step(b, par_, f, has_next, has_next2):
                    for h in range(NH):
                        weights(b, h)
                        if has_next2 and h == QUANT_HEAD:
                            copy_quant(b + 2)
                        if has_next2 and h >= STACK_LAG:
                            scale_stack(b + 2, h - STACK_LAG)
                    if has_next2:
                        for j in range(NH - STACK_LAG, 2 * NG):
                            scale_stack(b + 2, j)
                    if f is not None:
                        for i in range(3):
                            gelu(f, i)
                    for g in range(NG):
                        if has_next:
                            shift(b + 1, 1 - par_, g)
                        if f is not None and 3 + g < HT1:
                            gelu(f, 3 + g)
                    split_high(b)

                nc.scalar.preload_act_table_set(GELU)
                act.wait_ge(qscale_ready.sem, qscale_ready.nth(0))
                for b in range(2):
                    copy_quant(b)
                    for j in range(2 * NG):
                        scale_stack(b, j)
                for g in range(NG):
                    shift(0, 0, g)
                step(0, 0, None, True, True)
                step(1, 1, 0, True, True)
                with act.Fori(2, B - 2, 2) as b:
                    step(b, 0, b - 1, True, True)
                    step(b + 1, 1, b, True, True)
                step(B - 2, 0, B - 3, True, False)
                step(B - 1, 1, B - 2, False, False)
                for i in range(HT1):
                    gelu(B - 1, i)

            @block.vector
            def _(dve):
                def quantise(b, first, end):
                    for k in range(first, end):
                        if k == 0:
                            dve.wait_ge(qx_landed.sem, qx_landed.nth(b))
                            dve.wait_ge(stat_ready.sem, stat_ready.nth(b))
                            for t in range(NT):
                                last = nc.vector.tensor_scalar(qx[:, t, :], h1[:, t, :], mvq[:, t, 0:1], rstdq[:, t:t + 1],
                                                               ALU.subtract, ALU.mult)
                            last.then_inc(xq_ready.sem, 1)
                        if k == 1:
                            dve.wait_ge(xq_ready.sem, xq_ready.nth(b, 1))
                            nc.vector.tensor_scalar(qx[:], qx[:], qinv[:], 127.0, ALU.mult, ALU.min).then_inc(xq_ready.sem, 1)
                        if k == 2:
                            dve.wait_ge(xq_ready.sem, xq_ready.nth(b, 2))
                            nc.vector.tensor_scalar(qx[:], qx[:], -128.0, ROUND, ALU.max, ALU.add).then_inc(xq_ready.sem, 1)
                        if k == 3:
                            dve.wait_ge(xq_ready.sem, xq_ready.nth(b, 3))
                            nc.vector.tensor_scalar(qnat[:], qx[:], ROUND, None, ALU.subtract).then_inc(qnat_ready.sem, 1)

                def copy_quant(b):
                    dve.wait_ge(qTa_ready.sem, qTa_ready.nth(b))
                    nc.vector.tensor_copy(qT_b[HALF:P], qT_b[0:HALF]).then_inc(qTb_ready.sem, 1)

                def stack_parts(b, par_, j, readers):
                    term = K_TERMQ if j % 2 == 0 else K_TERMK
                    dve.wait_ge(sfull_ready.sem, sfull_ready.nth(b, j + 1))
                    if readers is not None:
                        dve.wait_ge(sT_psum.sem, sT_psum.nth(readers, NT * 2 * (j // 2 + 1)))
                    nc.vector.scalar_tensor_tensor(stacks[par_][:, stack_at(j), :], shi[:, j % 2, :], cst[:, term:term + 1],
                                                   sfull[:, j % 2, :], ALU.mult, ALU.add).then_inc(stack_ready.sem, 1)

                def scale_values(b, par_):
                    dve.wait_ge(v1_psum.sem, v1_psum.nth(b))
                    for t in range(NT):
                        last = nc.vector.scalar_tensor_tensor(
                            v1[par_][t].rearrange("p (h c) -> p h c", c=P)[:, :, 0:DH],
                            V3[:, t, 0:D].rearrange("p (h c) -> p h c", c=DH), qscale[:],
                            par[:, V_BV:V_BV + D].rearrange("p (h c) -> p h c", c=DH), ALU.mult, ALU.add)
                    last.then_inc(v1_ready.sem, 1)

                def maxima(b, h, first=0, end=NT):
                    for t in range(first, end):
                        n = h * NT + t
                        dve.wait_ge(s_psum.sem, s_psum.nth(b, n + 1))
                        nc.vector.tensor_reduce(negmax[:, t * NH + h:t * NH + h + 1], S[n % 2], AX.X, ALU.max,
                                                negate=True).then_inc(max_ready.sem, 1)

                def maxima_parts(b):
                    dve.wait_ge(max_ready.sem, max_ready.nth(b))
                    nc.vector.tensor_scalar(nmf[:], negmax[:], 1.0 / MAXSCALE, None, ALU.mult).then_inc(nm_step.sem, 1)
                    dve.wait_ge(nm_step.sem, nm_step.nth(b, 1))
                    nc.vector.tensor_copy(nm_parts[0], nmf[:]).then_inc(nm_step.sem, 1)
                    dve.wait_ge(nm_step.sem, nm_step.nth(b, 2))
                    nc.vector.tensor_tensor(nmr[:], nmf[:], nm_parts[0], ALU.subtract).then_inc(nm_step.sem, 1)
                    dve.wait_ge(nm_step.sem, nm_step.nth(b, 3))
                    nc.vector.tensor_copy(nm_parts[1], nmr[:]).then_inc(nm_step.sem, 1)
                    dve.wait_ge(nm_step.sem, nm_step.nth(b, 4))
                    nc.vector.tensor_tensor(nm_parts[2], nmr[:], nm_parts[1], ALU.subtract).then_inc(nm_step.sem, 1)

                def sums(b, g, t):
                    dve.wait_ge(pv_done.sem, pv_done.nth(b, (g + 1) * CH4))
                    if g > 0 and t == 0:
                        dve.wait_ge(cx_ready.sem, cx_ready.nth(b, g))
                    nc.vector.reciprocal(csum[0:HALF, cols(t)], CT[g % 2][HALF:P, cols(t)]).then_inc(csum_ready.sem, 1)

                def context(b, g):
                    dve.wait_ge(csum_ready.sem, csum_ready.nth(b, (g + 1) * NT))
                    dst = hnT_b[:] if g == 2 else hnT_a[g * HALF:(g + 1) * HALF]
                    nc.vector.tensor_tensor(dst, CT[g % 2][0:HALF], csum[0:HALF], ALU.mult).then_inc(cx_ready.sem, 1)

                def add_attention(b, par_):
                    dve.wait_ge(wo1_psum.sem, wo1_psum.nth(b))
                    dve.wait_ge(hbo_ready.sem, hbo_ready.nth(b))
                    nc.vector.tensor_tensor(h4[par_][:], F3[:, :, 0:D], hbo[:], ALU.add).then_inc(h4_ready.sem, 1)
                    dve.wait_ge(h4_ready.sem, h4_ready.nth(b))
                    for t in range(NT):
                        last = nc.vector.bn_stats(st[:, t, :], h4[par_][:, t, :])
                    last.then_inc(ln4_stat.sem, 1)
                    dve.wait_ge(ln4_stat.sem, ln4_stat.nth(b, 1))
                    stand(dve)
                    for t in range(NT):
                        last = nc.vector.bn_aggr(mv[:, t, :], st[:, t, :])
                    last.then_inc(ln4_stat.sem, 1)

                def normalise(b, par_):
                    dve.wait_ge(ln4_rstd.sem, ln4_rstd.nth(b))
                    for t in range(NT):
                        last = nc.vector.tensor_scalar(xn[:, t, :], h4[par_][:, t, :], mv[:, t, 0:1], rstd[:, t:t + 1],
                                                       ALU.subtract, ALU.mult)
                    last.then_inc(xn4_ready.sem, 1)

                def split_low(b):
                    dve.wait_ge(x4_hi.sem, x4_hi.nth(b, 1))
                    nc.vector.tensor_tensor(ffn_x[1][:], F[0][:, 0:N], ffn_x[0][:], ALU.subtract).then_inc(x4_lo.sem, 1)
                    dve.wait_ge(x4_hi.sem, x4_hi.nth(b, 2))
                    nc.vector.tensor_tensor(ffn_x[2][HALF:P], F[1][0:HALF, 0:N], ffn_x[2][0:HALF],
                                            ALU.subtract).then_inc(x4_lo.sem, 1)

                def add_ffn(b, par_):
                    dve.wait_ge(out_done.sem, out_done.nth(b))
                    dve.wait_ge(out_stored.sem, out_stored.before(b))
                    nc.vector.tensor_tensor(ho[:], W3[:, :, 0:D], h4[par_][:], ALU.add).then_inc(ho_ready.sem, 1)

                def step(b, par_, before, has_next, has_next2):
                    for h in range(NH):
                        if has_next2 and h == 1:
                            for t in range(NT):
                                maxima(b + 1, h, t, t + 1)
                                quantise(b + 2, t + 1, t + 2)
                        elif has_next and h == 0:
                            if before is not None:
                                add_ffn(before, par_)
                            maxima(b + 1, h)
                        elif has_next:
                            maxima(b + 1, h)
                        if not has_next and h == 0:
                            add_ffn(before, par_)
                        if has_next2 and h == 0:
                            quantise(b + 2, 0, 1)
                        if has_next2 and h == QUANT_HEAD:
                            copy_quant(b + 2)
                        if has_next2 and h > STACK_LAG:
                            stack_parts(b + 2, par_, h - STACK_LAG - 1, b)
                        for g in range(2):
                            t = h - (g + 1) * CH4 - 1
                            if 0 <= t < NT:
                                sums(b, g, t)
                            if t == NT - 1:
                                context(b, g)
                    if has_next2:
                        stack_parts(b + 2, par_, NH - STACK_LAG - 1, b)
                    for t in range(NT):
                        sums(b, 2, t)
                        if has_next2 and t < 2:
                            stack_parts(b + 2, par_, NH - STACK_LAG + t, b)
                    context(b, 2)
                    if has_next2:
                        stack_parts(b + 2, par_, 2 * NG - 1, b)
                    if has_next:
                        maxima_parts(b + 1)
                    if has_next2:
                        scale_values(b + 2, par_)
                    add_attention(b, par_)
                    normalise(b, par_)
                    split_low(b)

                dve.wait_ge(allmax_ready.sem, allmax_ready.nth(0))
                nc.vector.tensor_scalar(qscale[:], allmax[:], 1.0 / 127.0, 1e-8, ALU.mult, ALU.max).then_inc(qscale_ready.sem, 1)
                dve.wait_ge(qscale_ready.sem, qscale_ready.nth(0, 1))
                nc.vector.reciprocal(qinv[:], qscale[:]).then_inc(qscale_ready.sem, 1)
                dve.wait_ge(qscale_ready.sem, qscale_ready.nth(0))
                quantise(0, 0, 4)
                copy_quant(0)
                for j in range(2 * NG):
                    stack_parts(0, 0, j, None)
                    if j == 1:
                        quantise(1, 0, 4)
                dve.wait_ge(ones_ready.sem, ones_ready.nth(0))
                scale_values(0, 0)
                copy_quant(1)
                for h in range(NH):
                    maxima(0, h)
                    if h > 0:
                        stack_parts(1, 1, h - 1, None)
                stack_parts(1, 1, NH - 1, None)
                maxima_parts(0)
                scale_values(1, 1)
                step(0, 0, None, True, True)
                step(1, 1, None, True, True)
                with dve.Fori(2, B - 2, 2) as b:
                    step(b, 0, b - 2, True, True)
                    step(b + 1, 1, b - 1, True, True)
                step(B - 2, 0, B - 4, True, False)
                step(B - 1, 1, B - 3, False, False)
                add_ffn(B - 2, 0)
                add_ffn(B - 1, 1)


def kernel(x, L0_attn_Wq, L0_attn_Wk, L0_attn_Wv, L0_attn_Wf, L0_attn_bf, L0_attn_Wo, L0_attn_gamma, L0_attn_beta,
           L0_ffn_router_w, L0_ffn_w_gate, L0_ffn_w_up, L0_ffn_w_down, L0_ffn_ws_gate, L0_ffn_ws_up, L0_ffn_ws_down,
           L0_ffn_sg_w, L0_ffn_sg_b, L1_attn_Wq, L1_attn_bq, L1_attn_Wk, L1_attn_bk, L1_attn_Wv, L1_attn_bv,
           L1_attn_Wo, L1_attn_bo, L1_ffn_in_weight, L1_ffn_in_bias, L1_ffn_out_weight):
    import numpy as np
    import concourse.bacc as bacc
    from concourse.bass_utils import run_bass_kernel_spmd

    def f(a):
        return np.asarray(a)

    def rows(w):
        w = f(w)
        return np.ascontiguousarray(w[0:P]), np.concatenate([w[P:D], w[P:D]], axis=0)

    gate = f(L0_ffn_w_gate).transpose(1, 0, 2).reshape(D, E0 * D)
    up = f(L0_ffn_w_up).transpose(1, 0, 2).reshape(D, E0 * D)
    gate = np.concatenate([gate, f(L0_ffn_ws_gate)], axis=1)
    up = np.concatenate([up, f(L0_ffn_ws_up)], axis=1)
    cols = [f(L0_attn_Wq), f(L0_attn_Wk), f(L0_attn_Wf), f(L0_attn_Wf), f(L0_attn_Wv), f(L0_ffn_router_w),
            f(L0_ffn_sg_w), np.zeros((D, RW - E0 - 1), np.float32)]
    for i in range(HT0):
        cols += [gate[:, i * P:(i + 1) * P], up[:, i * P:(i + 1) * P]]
    cols.append(f(L1_ffn_in_weight).T)
    w_a, w_b = rows(np.concatenate(cols, axis=1))

    def stack(w):
        w = f(w).reshape(w.shape[0], NH, 1, DH)
        return np.concatenate([w, w, w, np.zeros_like(w)], axis=2).reshape(w.shape[0], NH * HALF)

    wq_a, wq_b = rows(np.concatenate([stack(L1_attn_Wq), stack(L1_attn_Wk), f(L1_attn_Wv)], axis=1))

    def tiles(w):
        return np.ascontiguousarray(f(w).reshape(-1, P, D).transpose(1, 0, 2))

    w_down0 = tiles(np.concatenate([f(L0_ffn_w_down).reshape(E0 * D, D), f(L0_ffn_ws_down)], axis=0))
    w_out1 = tiles(L1_ffn_out_weight)
    w_o = np.zeros((P, 4, D), np.float32)
    for i, w in enumerate((f(L0_attn_Wo), f(L1_attn_Wo))):
        w_o[:, 2 * i] = w[0:P]
        w_o[0:HALF, 2 * i + 1] = w[P:D]

    r = np.arange(P)
    consts = np.zeros((P, KCOLS), np.float32)
    consts[:, K_ID:K_ID + P] = np.eye(P)
    consts[:, K_MASK:K_MASK + P] = r[None, :] >= r[:, None]
    consts[:, K_SGN] = np.where(r < M0, -1, 1)
    consts[:, K_TERMQ] = np.where(r % HALF < DH, -1, 0)
    consts[:, K_TERMK] = np.where((r % HALF >= DH) & (r % HALF < 2 * DH), -1, 0)
    consts[:, K_QSC] = 127 * BITS
    consts[:, K_IOTA:K_IOTA + E0] = np.arange(E0)

    params = np.zeros((P, VCOLS), np.float32)
    params[:, V_BF] = np.concatenate([f(L0_attn_bf), f(L0_attn_bf)])
    params[:, V_GA], params[0:HALF, V_GB] = f(L0_attn_gamma)[0:P], f(L0_attn_gamma)[P:D]
    params[:, V_BA], params[0:HALF, V_BB] = f(L0_attn_beta)[0:P], f(L0_attn_beta)[P:D]
    params[:, V_SG] = f(L0_ffn_sg_b)[0]
    params[:, V_IN:V_IN + HT1] = f(L1_ffn_in_bias).reshape(HT1, P).T
    params[:, V_BQ:V_BQ + NG] = stack(f(L1_attn_bq)[None]).reshape(NG, P).T
    params[:, V_BK:V_BK + NG] = stack(f(L1_attn_bk)[None]).reshape(NG, P).T
    for i in range(3):
        params[48 + i::HALF, V_BK:V_BK + NG] = MAXSCALE
    params[:, V_BV:V_BV + D] = f(L1_attn_bv)[None]
    params[:, V_BO:V_BO + D] = f(L1_attn_bo)[None]

    sel = np.zeros((32, NGATE, P), np.float32)
    for i in range(NGATE):
        which = (i * P + r) // D if i < RT0 else np.full(P, E0)
        for part in range(3):
            sel[part * 9 + which, i, r] = 1

    nc = bacc.Bacc("TRN2", target_bir_lowering=False, num_devices=1)
    x = f(x)
    arrays, args = {}, []
    for name, a in (("x", x), ("w_a", w_a), ("w_b", w_b), ("wq_a", wq_a), ("wq_b", wq_b), ("w_down0", w_down0),
                    ("w_out1", w_out1), ("w_o", w_o), ("consts", consts), ("params", params), ("sel", sel)):
        arrays[name] = np.ascontiguousarray(a)
        args.append(nc.dram_tensor(name, a.shape, mybir.dt.from_np(a.dtype), kind="ExternalInput").ap())
    args.append(nc.dram_tensor("out", (x.shape[0], N, D), F32, kind="ExternalOutput").ap())
    tower(nc, *args)
    r = run_bass_kernel_spmd(nc, [arrays], core_ids=[0])
    return r.results[0]["out"]
```
